# Optimizing a Trainium2 kernel written in Bass

```python
import numpy as np
import jax
import jax.numpy as jnp

def _softmax(x, axis=-1):
    return jax.nn.softmax(x, axis=axis)

def _gelu(x):
    return jax.nn.gelu(x, approximate=True)

def _silu(x):
    return jax.nn.silu(x)

def _sigmoid(x):
    return jax.nn.sigmoid(x)

def _layernorm(x, axis=-1, eps=1e-05):
    m = jnp.mean(x, axis=axis, keepdims=True)
    v = jnp.var(x, axis=axis, keepdims=True)
    return (x - m) / jnp.sqrt(v + eps)

def _scatter_add(tgt, idx, src, axis=0):
    return tgt.at[idx].add(src)

def _segment_sum(src, seg, n):
    return jax.ops.segment_sum(src, seg, n)
kernel_name = 'mk_xattn_seq_d2_seqx_r8_d05f78'

def setup_inputs(seed: int=0):
    np.random.seed(seed)
    _w = jnp.asarray

    def _rec_inputs():
        import jax
        import jax.numpy as jnp
        _rk = jax.random.key(seed)
        x = -0.000719 + 1.001 * jax.random.normal(jax.random.fold_in(_rk, 1), (16, 256, 160), jnp.float32)
        _lenS = 256 - jax.random.randint(jax.random.fold_in(_rk, 7), (16,), 0, max(1, 256 // 4) + 1, jnp.int32)
        _lenS2 = 64 - jax.random.randint(jax.random.fold_in(_rk, 8), (16,), 0, max(1, 64 // 4) + 1, jnp.int32)
        _ctx_2048P = jax.random.normal(jax.random.fold_in(_rk, 11), (16, 16, 256), jnp.float32)
        _ctx_2048c = jax.random.dirichlet(jax.random.fold_in(_rk, 511), 0.3 * jnp.ones((16,), jnp.float32), (16, 64))
        _ctx_2048t = jnp.einsum('bsk,bkd->bsd', _ctx_2048c, _ctx_2048P)
        _ctx_2048t = _ctx_2048t * jax.lax.rsqrt(jnp.mean(jnp.square(_ctx_2048t)) + 1e-12) * 0.953939
        ctx_2048 = 0.00257118 + 0.99863 * (_ctx_2048t + 0.3 * jax.random.normal(jax.random.fold_in(_rk, 611), (16, 64, 256), jnp.float32))
        fside_S_0 = jax.random.uniform(jax.random.fold_in(_rk, 12), (256,), jnp.float32, 0.0, 0.999706)
        return (x, ctx_2048, fside_S_0)
    x, ctx_2048, fside_S_0 = _rec_inputs()

    def _L0_xattn_setup():
        import jax, jax.numpy as jnp
        import numpy as np
        HEADS = 20
        NUM_TOKENS = 4
        IP_SCALE = 1.0
        SEM_SCALE = 0.5
        RESCALE = 1.0
        EPS = 1e-12

        def _l2norm(x, axis=-1):
            n = jnp.sqrt(jnp.sum(x * x, axis=axis, keepdims=True))
            return x / jnp.maximum(n, EPS)
        key = jax.random.key(seed)
        ks = jax.random.split(key, 10)
        B, S, C = (2, 128, 160)
        T, E = (81, 256)
        inp = {'hidden_states': jax.random.normal(ks[0], (B, S, C), jnp.float32), 'encoder_hidden_states': jax.random.normal(ks[1], (B, T, E), jnp.float32), 'spatial_mask': jax.random.uniform(ks[2], (S,), jnp.float32), 'W_q': jax.random.normal(ks[3], (C, C), jnp.float32) * C ** (-0.5), 'W_k': jax.random.normal(ks[4], (E, C), jnp.float32) * E ** (-0.5), 'W_v': jax.random.normal(ks[5], (E, C), jnp.float32) * E ** (-0.5), 'W_k_ip': jax.random.normal(ks[6], (E, C), jnp.float32) * E ** (-0.5), 'W_v_ip': jax.random.normal(ks[7], (E, C), jnp.float32) * E ** (-0.5), 'W_out': jax.random.normal(ks[8], (C, C), jnp.float32) * C ** (-0.5), 'b_out': jnp.zeros((C,), jnp.float32)}
        return inp
    _L0_xattn_all = _L0_xattn_setup()
    _L0_xattn_in = {k: v for k, v in _L0_xattn_all.items() if k in ('W_q', 'W_k', 'W_v', 'W_k_ip', 'W_v_ip', 'W_out', 'b_out')}
    del _L0_xattn_all

    def _L1_xattn_setup():
        import jax, jax.numpy as jnp
        import numpy as np
        NUM_HEADS = 20
        TEXT_LEN = 77
        IP_SCALE = 1.0

        def _attend(q, k, v, sm_scale):
            scores = jnp.einsum('bhsd,bhld->bhsl', q, k) * sm_scale
            probs = jax.nn.softmax(scores, axis=-1)
            return jnp.einsum('bhsl,bhld->bhsd', probs, v)

        def _split_heads(x, h):
            b, s, c = x.shape
            return x.reshape(b, s, h, c // h).transpose(0, 2, 1, 3)

        def _merge_heads(x):
            b, h, s, d = x.shape
            return x.transpose(0, 2, 1, 3).reshape(b, s, h * d)
        key = jax.random.key(seed)
        ks = jax.random.split(key, 8)
        B, S, C, CC, L = (8, 512, 160, 256, TEXT_LEN + 4)
        sd_q = 1.0 / np.sqrt(C)
        sd_kv = 1.0 / np.sqrt(CC)
        return {'hidden_states': jax.random.normal(ks[0], (B, S, C), jnp.float32), 'encoder_hidden_states': jax.random.normal(ks[1], (B, L, CC), jnp.float32), 'Wq': jax.random.normal(ks[2], (C, C), jnp.float32) * sd_q, 'Wk': jax.random.normal(ks[3], (C, CC), jnp.float32) * sd_kv, 'Wv': jax.random.normal(ks[4], (C, CC), jnp.float32) * sd_kv, 'Wk_ip': jax.random.normal(ks[5], (C, CC), jnp.float32) * sd_kv, 'Wv_ip': jax.random.normal(ks[6], (C, CC), jnp.float32) * sd_kv, 'Wo': jax.random.normal(ks[7], (C, C), jnp.float32) * sd_q, 'bo': jnp.zeros((C,), jnp.float32)}
    _L1_xattn_all = _L1_xattn_setup()
    _L1_xattn_in = {k: v for k, v in _L1_xattn_all.items() if k in ('Wq', 'Wk', 'Wv', 'Wk_ip', 'Wv_ip', 'Wo', 'bo')}
    del _L1_xattn_all
    return {'x': x, 'ctx_2048': ctx_2048, 'fside_S_0': fside_S_0, 'L0_xattn_W_q': _L0_xattn_in['W_q'], 'L0_xattn_W_k': _L0_xattn_in['W_k'], 'L0_xattn_W_v': _L0_xattn_in['W_v'], 'L0_xattn_W_k_ip': _L0_xattn_in['W_k_ip'], 'L0_xattn_W_v_ip': _L0_xattn_in['W_v_ip'], 'L0_xattn_W_out': _L0_xattn_in['W_out'], 'L0_xattn_b_out': _L0_xattn_in['b_out'], 'L1_xattn_Wq': _L1_xattn_in['Wq'], 'L1_xattn_Wk': _L1_xattn_in['Wk'], 'L1_xattn_Wv': _L1_xattn_in['Wv'], 'L1_xattn_Wk_ip': _L1_xattn_in['Wk_ip'], 'L1_xattn_Wv_ip': _L1_xattn_in['Wv_ip'], 'L1_xattn_Wo': _L1_xattn_in['Wo'], 'L1_xattn_bo': _L1_xattn_in['bo']}

def reference(x, ctx_2048, fside_S_0, L0_xattn_W_q, L0_xattn_W_k, L0_xattn_W_v, L0_xattn_W_k_ip, L0_xattn_W_v_ip, L0_xattn_W_out, L0_xattn_b_out, L1_xattn_Wq, L1_xattn_Wk, L1_xattn_Wv, L1_xattn_Wk_ip, L1_xattn_Wv_ip, L1_xattn_Wo, L1_xattn_bo):
    import jax
    import jax.numpy as jnp

    def _L0_xattn_ref(hidden_states, encoder_hidden_states, spatial_mask, W_q, W_k, W_v, W_k_ip, W_v_ip, W_out, b_out):
        import jax, jax.numpy as jnp
        import numpy as np
        HEADS = 20
        NUM_TOKENS = 4
        IP_SCALE = 1.0
        SEM_SCALE = 0.5
        RESCALE = 1.0
        EPS = 1e-12

        def _l2norm(x, axis=-1):
            n = jnp.sqrt(jnp.sum(x * x, axis=axis, keepdims=True))
            return x / jnp.maximum(n, EPS)
        B, S, C = hidden_states.shape
        H = HEADS
        Dh = C // H
        attn_scale = Dh ** (-0.5)
        residual = hidden_states
        text_ehs = encoder_hidden_states[:, :-NUM_TOKENS]
        ip_ehs = encoder_hidden_states[:, -NUM_TOKENS:]

        def heads(x):
            return x.reshape(B, -1, H, Dh).transpose(0, 2, 1, 3)
        q = heads(hidden_states @ W_q)
        k_t = heads(text_ehs @ W_k)
        v_t = heads(text_ehs @ W_v)
        scores_t = jnp.einsum('bhsd,bhtd->bhst', q, k_t) * attn_scale
        probs_t = jax.nn.softmax(scores_t, axis=-1)
        text_out = jnp.einsum('bhst,bhtd->bhsd', probs_t, v_t)
        text_out = text_out.transpose(0, 2, 1, 3).reshape(B, S, C)
        k_ip = heads(ip_ehs @ W_k_ip)
        v_ip = heads(ip_ehs @ W_v_ip)
        attn_scores = jnp.einsum('bhsd,bhnd->bhsn', q, k_ip) * attn_scale
        qsem = jnp.einsum('bhst,bte->bhse', probs_t, text_ehs)
        qsem = _l2norm(qsem)
        ip_n = _l2norm(ip_ehs)
        sem = jnp.einsum('bhse,bne->bhsn', qsem, ip_n)
        sem = jax.lax.stop_gradient(sem)
        fused = attn_scores + SEM_SCALE * sem
        probs_ip = jax.nn.softmax(fused, axis=-1)
        probs_ip = probs_ip * spatial_mask[None, None, :, None]
        ip_out = jnp.einsum('bhsn,bhnd->bhsd', probs_ip, v_ip)
        ip_out = ip_out.transpose(0, 2, 1, 3).reshape(B, S, C)
        out = text_out + IP_SCALE * ip_out
        out = out @ W_out + b_out
        out = out + residual
        return out / RESCALE

    def _L1_xattn_ref(hidden_states, encoder_hidden_states, Wq, Wk, Wv, Wk_ip, Wv_ip, Wo, bo):
        import jax, jax.numpy as jnp
        import numpy as np
        NUM_HEADS = 20
        TEXT_LEN = 77
        IP_SCALE = 1.0

        def _attend(q, k, v, sm_scale):
            scores = jnp.einsum('bhsd,bhld->bhsl', q, k) * sm_scale
            probs = jax.nn.softmax(scores, axis=-1)
            return jnp.einsum('bhsl,bhld->bhsd', probs, v)

        def _split_heads(x, h):
            b, s, c = x.shape
            return x.reshape(b, s, h, c // h).transpose(0, 2, 1, 3)

        def _merge_heads(x):
            b, h, s, d = x.shape
            return x.transpose(0, 2, 1, 3).reshape(b, s, h * d)
        residual = hidden_states
        B, S, C = hidden_states.shape
        H = NUM_HEADS
        D = C // H
        sm_scale = 1.0 / jnp.sqrt(jnp.asarray(D, hidden_states.dtype))
        text = encoder_hidden_states[:, :TEXT_LEN, :]
        ip = encoder_hidden_states[:, TEXT_LEN:, :]
        q = _split_heads(hidden_states @ Wq.T, H)
        k = _split_heads(text @ Wk.T, H)
        v = _split_heads(text @ Wv.T, H)
        out_text = _merge_heads(_attend(q, k, v, sm_scale))
        k_ip = _split_heads(ip @ Wk_ip.T, H)
        v_ip = _split_heads(ip @ Wv_ip.T, H)
        out_ip = _merge_heads(_attend(q, k_ip, v_ip, sm_scale))
        out = out_text + IP_SCALE * out_ip
        out = out @ Wo.T + bo
        return out + residual
    x = _L0_xattn_ref(x, ctx_2048, fside_S_0, L0_xattn_W_q, L0_xattn_W_k, L0_xattn_W_v, L0_xattn_W_k_ip, L0_xattn_W_v_ip, L0_xattn_W_out, L0_xattn_b_out)
    x = _L1_xattn_ref(x, ctx_2048, L1_xattn_Wq, L1_xattn_Wk, L1_xattn_Wv, L1_xattn_Wk_ip, L1_xattn_Wv_ip, L1_xattn_Wo, L1_xattn_bo)
    return x

_drawn_inputs = setup_inputs


def setup_inputs(seed=0):
    import zlib

    import numpy as np

    out = dict(_drawn_inputs(seed))
    spreads = {'L0_xattn_b_out': (0.0, 0.1), 'L1_xattn_bo': (0.0, 0.1)}
    factors = {}
    for name, (base, spread) in spreads.items():
        noise = np.random.default_rng([zlib.crc32(name.encode()), seed]).standard_normal(out[name].shape)
        drawn = base * np.exp(spread * noise) if base else spread * noise
        out[name] = jnp.asarray(drawn.astype(out[name].dtype))
    for name, factor in factors.items():
        out[name] = (out[name] * factor).astype(out[name].dtype)
    return out
```

```python
from contextlib import ExitStack

import numpy as np

import concourse.bass as bass
from concourse import mybir

F32 = mybir.dt.float32
BF16 = mybir.dt.bfloat16
ALU = mybir.AluOpType
ACT = mybir.ActivationFunctionType
AX_X = mybir.AxisListType.X

B, S, C, E, T = 16, 256, 160, 256, 64
H, D = 20, 8
N_IP = 4
PAIRS, R = H // 2, 2 * D
HC = C // 2
HP = PAIRS // 2
ROWS = B * S
NT = (T - N_IP, T)
M2 = (2 * NT[0], 2 * NT[1])
SCALE = float(D) ** -0.5
EPS2 = 1e-24
SEM_SCALE = 0.5

Q_PARTS = (0, 0, 0, 1, 1, 2)
K_PARTS = (0, 1, 2, 0, 1, 0)
KR = 16 * len(Q_PARTS)
KM = KR + 4
V_COLS, NUM0, SUM0, QUAD0, VW_COLS = 16, 16, 24, 26, 32
KE = 2
IP_ROW = 32
Z1 = IP_ROW + H * N_IP
STEPS_UNROLLED = 4
N_G = 2 * B

C_ID, C_KHH, C_MV0, C_MV1, C_MHH0, C_MHH1, C_QSEL, C_MVH, C_ONE, C_END = np.cumsum(
    [0, 128, 2, 16, 16, 2, 2, VW_COLS, 2 * H, 128]).tolist()


def constants():
    c = np.zeros((128, C_END), np.float32)
    c[:, C_ID:C_ID + 128] = np.eye(128)
    for p in range(HC):
        c[p, C_KHH + (p // HP) // D] = 1
    for layer, (mv, mhh) in enumerate(((C_MV0, C_MHH0), (C_MV1, C_MHH1))):
        for row in range(M2[layer]):
            hh = row // NT[layer]
            c[row, mv + hh * D:mv + hh * D + D] = 1
            c[row, mhh + hh] = 1
            if layer == 0:
                c[row, C_QSEL + QUAD0 + hh] = 1
    for half in range(2):
        for ch in range(HC):
            c[ch, C_MVH + half * H + (half * HC + ch) // D] = 1
    c[:, C_ONE:C_ONE + 128] = 1
    rows = np.zeros((2, 4, 128), np.float32)
    for layer in range(2):
        for part in range(2):
            for hh in range(2):
                rows[layer, 2 * part + hh, hh * NT[layer]:(hh + 1) * NT[layer]] = 1
    bf16 = mybir.dt.np(BF16)
    return c, rows.astype(bf16), np.eye(128).astype(bf16)


class At:

    def __init__(self, base, i=None):
        self.base, self.i = base, i

    def n(self, mul=1, add=0):
        v = self.base * mul + add
        return v if self.i is None else self.i * (STEPS_UNROLLED * mul) + v

    def block(self, mul=1, add=0):
        v = self.base // 2 * mul + add
        return v if self.i is None else self.i * (STEPS_UNROLLED // 2 * mul) + v

    def plus(self, k):
        return At(self.base + k, self.i)

    @property
    def layer(self):
        return self.base // B


def need(eng, sem, n):
    if not isinstance(n, int) or n > 0:
        eng.wait_ge(sem, n)


def fixed(eng, v):
    return v if isinstance(v, int) else eng.snap(v)


PE_STEP = [("st", 0, 0), ("st", 0, 1), ("q", 3, 0), ("u", 0, 0), ("ot", -1, 0), ("st", 0, 2), ("ot", -1, 1),
           ("u", 0, 1), ("pv", 0, 0), ("sc", 1, 0), ("sc", 1, 1), ("st", 0, 3), ("u", 0, 2), ("quad", 0, 0),
           ("sc", 1, 2), ("sc", 1, 3), ("st", 0, 4), ("u", 0, 3), ("pv", 0, 1), ("sc", 1, 4), ("vk", 1, 0),
           ("u", 0, 4), ("quad", 0, 1), ("pv", 0, 2), ("mt", 1, 0), ("zt", -1, 0), ("vw", 0, 0),
           ("quad", 0, 2), ("y", -1, 0)]
ACT_STEP = [("otev", -1, 0), ("exp", 0, 0), ("qh", 3, 0), ("exp", 0, 1), ("kh", 3, 0), ("qm", 3, 0), ("exp", 0, 2),
            ("rsq", -1, 0), ("exp", 0, 3), ("exp", 0, 4), ("ipe", -1, 0), ("km", 3, 0), ("mtev", 1, 0),
            ("ztev", -1, 0)]
DVE_STEP = [("qr", 3, 0), ("w", 0, 0), ("on", -1, 0), ("on", -1, 1), ("ipa", -1, 0), ("w", 0, 1), ("red", 1, 0),
            ("red", 1, 1), ("w", 0, 2), ("red", 1, 2), ("ipm", -1, 0), ("red", 1, 3), ("w", 0, 3), ("red", 1, 4), ("neg", 1, 0), ("ipr", -1, 0),
            ("vprep", 1, 0), ("w", 0, 4), ("wz", 0, 0), ("ysb", -1, 0)]
POOL_STEP = [("kmask", 3, 0), ("ql", 3, 0), ("ipb", -1, 0), ("kr", 3, 0), ("ipd", -1, 0), ("vpb", 0, 0),
             ("ipz", -1, 0), ("kl", 3, 0)]
SP_STEP = [("cwd", 2, 0), ("kd", 2, 0), ("mtd", 1, 0), ("qd", 3, 0), ("outd", -1, 0)]
FILLS = ("q", "ot", "sc", "vk", "mt", "zt", "vw", "y")
LAYER0_ONLY = ("u", "quad", "vw", "w", "wz", "rsq", "ipe", "ipr", "ipa", "ipb", "ipm", "ipd", "vpb", "ipz")
LAYER1_ONLY = ("outd",)
BY_BLOCK = ("kh", "km", "kmask", "kr", "kl", "kd")
FIRST_STEP, LAST_STEP = -3, N_G
LOOPS = {1: 3, B + 1: 3}


def present(what, g):
    if not 0 <= g < N_G or (what in BY_BLOCK and g % 2):
        return False
    return not ((what in LAYER0_ONLY and g >= B) or (what in LAYER1_ONLY and g < B))


def fill_order():
    return [(w, t + d, k) for t in range(FIRST_STEP, LAST_STEP + 1) for w, d, k in PE_STEP
            if w in FILLS and present(w, t + d)]


def xattn_kernel(nc, xT, ctxT, ctx0, ctx1, side, WQ, WK, WKIP, WV, WVIP, WO0, WREM, WOP, WO1, BO,
                 consts, ones_rows, ident16, outT):
    order = fill_order()
    number = {f: n for n, f in enumerate(order)}

    with ExitStack() as stack:
        def sb(name, shape, dt=F32):
            return stack.enter_context(nc.sbuf_tensor(name, shape, dt))

        def sem(name):
            return stack.enter_context(nc.semaphore(name))

        cst = sb("cst", [128, C_END])
        id16 = sb("id16", [128, 128], BF16)
        wq = [sb(f"wq{n}", [HC, 2, C]) for n in range(2)]
        wk = [sb(f"wk{n}", [128, KE, C]) for n in range(2)]
        wkip, wvip = sb("wkip", [128, KE, C]), sb("wvip", [128, KE, C])
        wv1 = sb("wv1", [128, KE, C])
        wo0 = sb("wo0", [128, C])
        wrem = sb("wrem", [Z1, C])
        wop = sb("wop", [HC, 2, C])
        wo1 = sb("wo1", [HC, 2, C])
        bo = sb("bo", [HC, 2, 2])
        fside = sb("fside", [128, 2])
        x = sb("x", [HC, 2, ROWS])
        ca = sb("ca", [128, KE, B * T])
        kt = [sb(f"kt{n}", [HC, 2, B, T]) for n in range(2)]
        vipt = sb("vipt", [HC, 2, B, N_IP])
        ipsq = sb("ipsq", [128, KE, B * N_IP])
        inv = sb("inv", [128, 4, B * N_IP])
        simw = sb("simw", [M2[0], B, 2, N_IP])
        qp = sb("qp", [HC, 3, 2, 2 * S], BF16)
        qr = sb("qr", [HC, 2 * S])
        kmk = sb("kmk", [HC, 2, 2, 128])
        kp = sb("kp", [HC, 3, 2, 2, 128], BF16)
        krem = sb("krem", [HC, 2, 2, 128])
        qs = sb("qs", [128, 2, PAIRS, 2 * S], BF16)
        ks = [sb(f"ks{n}", [128, 2, PAIRS, 2, 128], BF16) for n in range(2)]
        mx = sb("mx", [128, 2, PAIRS, 2])
        mc = sb("mc", [128, 2, 2, 2, PAIRS], BF16)
        mt = sb("mt", [8 * PAIRS, 2, 128], BF16)
        ipraw = sb("ipraw", [128, 4, 2, PAIRS, 2 * N_IP])
        pt = sb("pt", [128, 2, PAIRS, S])
        wt = sb("wt", [M2[0], 2, PAIRS, S])
        vb = [sb(f"vb{n}", [M2[n], 2, PAIRS, VW_COLS]) for n in range(2)]
        sim8 = sb("sim8", [M2[0], 2, N_IP])
        gram = sb("gram", [M2[0], 2, M2[0]])
        cw = sb("cw", [128, 2, KE, M2[0] + T + C])
        cw1 = sb("cw1", [128, 2, KE, M2[1]])
        vpb = sb("vpb", [HC, 2, 2, Z1])
        wz = sb("wz", [Z1, 2, C])
        ots = sb("ots", [128, 3, S])
        rs = sb("rs", [128, 2, PAIRS, 2])
        stat = sb("stat", [128, 2, PAIRS, 12])
        z = sb("z", [128, 2, C + H * N_IP])
        zt = sb("zt", [128, 2, S])
        e40 = sb("e40", [128, 8, 2 * H])
        e160 = sb("e160", [128, 3, 2 * H, N_IP])

        ps = stack.enter_context(nc.psum_tensor("ps", [128, 8, 512], F32))

        w_in, c_in, k_in, rest_in = sem("w_in"), sem("c_in"), sem("k_in"), sem("rest_in")
        x_in = [sem(f"x_in{n}") for n in range(3)]
        rows_in = sem("rows_in")
        zeroed, vsum, sq_made = sem("zeroed"), sem("vsum"), sem("sq_made")
        setup_ps, setup_sb, inv_step, simw_made = sem("setup_ps"), sem("setup_sb"), sem("inv_step"), sem("simw_made")
        q_ps, q_h, q_r, q_m, q_l = (sem(f"q_{n}") for n in ("ps", "h", "r", "m", "l"))
        k_mask, k_h, k_r, k_m, k_l = (sem(f"k_{n}") for n in ("mask", "h", "r", "m", "l"))
        q_stacked = [sem(f"q_stacked{n}") for n in range(2)]
        k_stacked = sem("k_stacked")
        m_stacked = [sem(f"m_stacked{n}") for n in range(2)]
        cw_in = [sem(f"cw_in{n}") for n in range(2)]
        sc_ps, red_done, m_hi, m_lo, mt_ps, mt_sb = (
            sem(n) for n in ("sc_ps", "red_done", "m_hi", "m_lo", "mt_ps", "mt_sb"))
        st_ps, exp_done, u_ps, w_done, core_done = (sem(n) for n in ("st_ps", "exp_done", "u_ps", "w_done", "core_done"))
        vk_ps, v_made, sim_made, gram_made, simv_made = (
            sem(n) for n in ("vk_ps", "v_made", "sim_made", "gram_made", "simv_made"))
        vpb_made, vw_ps, wz_made = sem("vpb_made"), sem("vw_ps"), sem("wz_made")
        ot_sb, ot_ps, r_made, stat_made, z_made = (sem(n) for n in ("ot_sb", "ot_ps", "r_made", "stat_made", "z_made"))
        ip_least, ip_q2, ip_half, ip_rsq, ip_fused, ip_max, ip_less, ip_exp, ip_sum, ip_rec, ip_z = (
            sem(n) for n in ("ip_least", "ip_q2", "ip_half", "ip_rsq", "ip_fused", "ip_max", "ip_less", "ip_exp", "ip_sum",
                             "ip_rec", "ip_z"))
        pool_chain, act_chain = sem("pool_chain"), sem("act_chain")
        zt_ps, zt_sb, y_ps, y_sb, out_done = (sem(n) for n in ("zt_ps", "zt_sb", "y_ps", "y_sb", "out_done"))

        ident = cst[:, C_ID:C_ID + 128]

        def stats(lo, hi):
            return stat[:, :, :, lo:hi].rearrange("p t a c -> p (t a) c")

        def by_head(ap):
            return ap.rearrange("p (a h) -> p a h", h=2)

        def consumed(f, a):
            what, k = f[0], f[2]
            if what == "q":
                return q_r, a.n(1, 1)
            if what == "ot":
                return z_made, a.n(2, k + 1)
            if what == "sc":
                return red_done, a.n(6, 6 if k == 4 else k + 1)
            if what == "vk":
                return (gram_made if a.layer == 0 else v_made), a.n(1, 1)
            return {"mt": mt_sb, "zt": zt_sb, "vw": wz_made, "y": y_sb}[what], a.n(1, 1)

        def bank_of(what, a, k):
            return number[what, a.base, k] % 2

        def claim_bank(pe, what, a, k):
            base = a.base
            if a.i is None:
                n = number[what, base, k]
                if n >= 2:
                    f = order[n - 2]
                    pe.wait_ge(*consumed(f, At(f[1])))
                return n % 2
            n = number[what, base + STEPS_UNROLLED, k]
            f = order[n - 2]
            pe.wait_ge(*consumed(f, At(f[1] - STEPS_UNROLLED, a.i)))
            assert number[what, base, k] % 2 == n % 2
            return n % 2

        def run(step_list, stages, before_loop=None, after_step=None):
            def body(t):
                for what, d, k in step_list:
                    if present(what, t.base + d):
                        stages[what](t.plus(d), k)

            def program(eng):
                t = FIRST_STEP
                while t <= LAST_STEP:
                    if t in LOOPS:
                        if before_loop:
                            before_loop(t)
                        with eng.Fori(0, LOOPS[t]) as i:
                            for u in range(STEPS_UNROLLED):
                                body(At(t + u, i))
                        t += STEPS_UNROLLED * LOOPS[t]
                    else:
                        body(At(t))
                        if after_step and t in after_step:
                            after_step[t]()
                        t += 1
            return program

        block = stack.enter_context(nc.Block())

        @block.sync
        def _(sp):
            sp.dma_start(cst[:, :], consts).then_inc(w_in, 16)
            sp.dma_start(wq[0][:, :, :], WQ[0]).then_inc(w_in, 16)
            sp.dma_start(x[:, :, 0:2 * S], xT[:, :, 0:2 * S]).then_inc(x_in[0], 16)
            sp.dma_start(wkip[:, :, :], WKIP).then_inc(k_in, 16)
            sp.dma_start(id16[:, :], ident16).then_inc(rest_in, 16)
            for n in range(2):
                for slot in range(2):
                    for b2 in range(2):
                        sp.dma_start(ks[n][KR:KM, slot, :, b2, :],
                                     ones_rows[n].unsqueeze(1).broadcast_to([4, PAIRS, 128])).then_inc(rows_in, 16)
            sp.dma_start(x[:, :, 2 * S:4 * S], xT[:, :, 2 * S:4 * S]).then_inc(x_in[1], 16)
            for n in range(2):
                sp.dma_start(cw[:, n, :, M2[0] + T:], WV[0]).then_inc(rest_in, 16)
            sp.dma_start(wvip[:, :, :], WVIP).then_inc(k_in, 16)
            sp.dma_start(wop[:, :, :], WOP).then_inc(rest_in, 16)
            sp.dma_start(wrem[:, :], WREM).then_inc(rest_in, 16)
            sp.dma_start(fside[:, :], side).then_inc(rest_in, 16)
            sp.dma_start(wo0[:, :], WO0).then_inc(rest_in, 16)
            sp.dma_start(bo[:, :, :], BO).then_inc(rest_in, 16)
            sp.dma_start(wq[1][:, :, :], WQ[1]).then_inc(rest_in, 16)
            sp.dma_start(wo1[:, :, :], WO1).then_inc(rest_in, 16)
            sp.dma_start(wk[1][:, :, :], WK[1]).then_inc(rest_in, 16)
            sp.dma_start(wv1[:, :, :], WV[1]).then_inc(rest_in, 16)
            sp.dma_start(x[:, :, 4 * S:], xT[:, :, 4 * S:]).then_inc(x_in[2], 16)

            def load_context(a, _):
                n = a.base % 2
                dst, src, first = ((cw[:, n, :, 0:M2[0] + T], ctx0, 0) if a.layer == 0
                                   else (cw1[:, n, :, :], ctx1, B))
                batch = fixed(sp, a.n(1, -first))
                need(sp, vk_ps, a.n(1, -1))
                sp.dma_start(dst, src[bass.ds(batch, 1)].rearrange("o p k t -> (o p) k t")).then_inc(cw_in[n], 16)

            def store(a, _):
                c = fixed(sp, a.n(S, -ROWS))
                sp.wait_ge(y_sb, a.n(1, 1))
                sp.dma_start(outT[:, :, bass.ds(c, S)], x[:, :, bass.ds(c, S)]).then_inc(out_done, 16)

            def stack_keys(a, _):
                sp.wait_ge(k_l, a.block(1, 1))
                slot = a.base // 2 % 2
                for j, part in enumerate(K_PARTS):
                    for half in range(2):
                        sp.dma_start(ks[a.layer][16 * j:16 * j + 16, slot, half * HP:(half + 1) * HP, :, :],
                                     kp[:, part, half, :, :]).then_inc(k_stacked, 16)

            def stack_queries(a, _):
                half, slot = a.base % 2, a.base // 2 % 2
                sp.wait_ge(q_l, a.n(1, 1))
                for j, part in enumerate(Q_PARTS):
                    sp.dma_start(qs[16 * j:16 * j + 16, slot, half * HP:(half + 1) * HP, :],
                                 qp[:, part, half, :]).then_inc(q_stacked[half], 16)

            def stack_maxima(a, _):
                sp.wait_ge(mt_sb, a.n(1, 1))
                slot, b2 = a.base // 2 % 2, a.base % 2
                for tile in range(2):
                    c = b2 * S + tile * 128
                    sp.dma_start(qs[KR:KM, slot, :, c:c + 128],
                                 mt[4 * PAIRS * tile:4 * PAIRS * (tile + 1), b2, :]).then_inc(m_stacked[b2], 16)

            run(SP_STEP, {"cwd": load_context, "outd": store, "kd": stack_keys, "qd": stack_queries,
                          "mtd": stack_maxima})(sp)
            sp.wait_ge(out_done, 16 * B)

        @block.tensor
        def _(pe):
            def accumulate(out, pairs_, sem_=None, **kw):
                for n, (l, r) in enumerate(pairs_):
                    last = nc.tensor.matmul(out, l, r, start=(n == 0), stop=(n == len(pairs_) - 1), **kw)
                if sem_ is not None:
                    last.then_inc(sem_, 1)

            def project_keys(layer):
                for half in range(2):
                    for n in range(2):
                        accumulate(ps[0:HC, 2 + 2 * half + n, :],
                                   [(wk[layer][:, e, half * HC:(half + 1) * HC], ca[:, e, n * 512:(n + 1) * 512])
                                    for e in range(KE)], setup_ps)

            pe.wait_ge(c_in, 32)
            project_keys(0)
            ipc = ca[:, :, :].rearrange("p k (b t) -> p k b t", t=T)[:, :, :, T - N_IP:]
            pe.wait_ge(k_in, 32)
            for w, bank in ((wkip, 6), (wvip, 7)):
                for half in range(2):
                    accumulate(ps[0:HC, bank, half * 64:(half + 1) * 64],
                               [(w[:, e, half * HC:(half + 1) * HC], ipc[:, e]) for e in range(KE)], setup_ps)
            pe.wait_ge(w_in, 32)
            pe.wait_ge(sq_made, 1)
            accumulate(ps[0:128, 7, 128:192], [(cst[:, C_ONE:C_ONE + 128], ipsq[:, e, :]) for e in range(KE)], setup_ps)

            def late_setup():
                pe.wait_ge(setup_sb, 8)
                pe.wait_ge(rest_in, 16 * 12)
                project_keys(1)

            def q(a, _):
                half, lay = a.base % 2, a.layer
                if lay == 0:
                    if a.base == 0:
                        pe.wait_ge(w_in, 32)
                        pe.wait_ge(x_in[0], 16)
                    elif a.base == 2:
                        pe.wait_ge(x_in[1], 16)
                    elif a.base == 4:
                        pe.wait_ge(x_in[2], 16)
                else:
                    pe.wait_ge(y_sb, a.block(2, 2 - B))
                bank = claim_bank(pe, "q", a, 0)
                rows = bass.ds(a.block(2 * S, -lay * ROWS), 2 * S)
                accumulate(ps[0:HC, bank, :], [(wq[lay][:, h, half * HC:(half + 1) * HC], x[:, h, rows])
                                               for h in range(2)], q_ps)

            def sc(a, f):
                slot, b2 = a.base // 2 % 2, a.base % 2
                if f == 0:
                    for half in range(2):
                        pe.wait_ge(q_stacked[half], a.block(16 * len(Q_PARTS), 16 * len(Q_PARTS)))
                    pe.wait_ge(k_stacked, a.block(32 * len(K_PARTS), 32 * len(K_PARTS)))
                bank = claim_bank(pe, "sc", a, f)
                units = [(f // 2, 4 * (f % 2) + n) for n in range(4)] if f < 4 else [(n // 2, 8 + n % 2) for n in range(4)]
                for n, (tile, pair) in enumerate(units):
                    c = b2 * S + tile * 128
                    last = nc.tensor.matmul(ps[:, bank, n * 128:(n + 1) * 128], qs[0:KR, slot, pair, c:c + 128],
                                            ks[a.layer][0:KR, slot, pair, b2, :], start=True, stop=True)
                last.then_inc(sc_ps, 1)

            def mt_(a, _):
                pe.wait_ge(m_lo, a.n(1, 1))
                if a.base == 0:
                    pe.wait_ge(rest_in, 16 * 12)
                bank = claim_bank(pe, "mt", a, 0)
                nc.tensor.transpose(ps[0:8 * PAIRS, bank, 0:64].bitcast(BF16),
                                    mc[:, :, :, :, :].rearrange("p t a b c -> p (t a b c)"), id16[:, :]).then_inc(mt_ps, 1)

            def st(a, c):
                slot, b2, m = a.base // 2 % 2, a.base % 2, M2[a.layer]
                if c == 0:
                    pe.wait_ge(m_stacked[b2], a.block(32, 32))
                    if a.base in (0, B):
                        pe.wait_ge(rows_in, 16 * 8)
                if a.base == 0 and c == 0:
                    pe.wait_ge(setup_sb, 12)
                need(pe, exp_done, a.n(5, c - 1))
                for n in range(2):
                    pair = 2 * c + n
                    last = nc.tensor.matmul(ps[0:m, 2 + (a.base + c) % 2, n * S:(n + 1) * S],
                                            ks[a.layer][0:KM, slot, pair, b2, 0:m],
                                            qs[0:KM, slot, pair, b2 * S:(b2 + 1) * S], start=True, stop=True)
                last.then_inc(st_ps, 1)

            def u(a, c):
                if c == 0:
                    pe.wait_ge(gram_made, a.n(1, 1))
                pe.wait_ge(exp_done, a.n(5, c + 1))
                need(pe, w_done, a.n(5, c - 1))
                nc.tensor.matmul(ps[0:M2[0], 4 + (a.base + c) % 2, :], gram[:, a.base % 2, :],
                                 pt[0:M2[0], a.base % 2, 2 * c:2 * c + 2, :].rearrange("p a b -> p (a b)"),
                                 start=True, stop=True).then_inc(u_ps, 1)

            def out_of(pair):
                j, grp = pair % 4, pair // 4
                return ps[32 * j:32 * j + VW_COLS, 6 + grp // 2, (grp % 2) * S:(grp % 2 + 1) * S]

            def group(grp):
                return range(4 * grp, min(4 * grp + 4, PAIRS))

            def pv(a, grp):
                if grp == 0:
                    need(pe, ot_sb, a.n(1, 0))
                    if a.base == 0:
                        pe.wait_ge(setup_sb, 12)
                    pe.wait_ge(v_made if a.layer else simv_made, a.n(1, 1))
                    if a.base in (0, B):
                        pe.wait_ge(vsum, 4)
                pe.wait_ge(exp_done, a.n(5, (2, 4, 5)[grp]))
                m = M2[a.layer]
                for pair in group(grp):
                    last = nc.tensor.matmul(out_of(pair), vb[a.layer][:, a.base % 2, pair, :],
                                            pt[0:m, a.base % 2, pair, :], start=(grp != 1),
                                            stop=(a.layer == 1), skip_group_check=True)
                if grp == 2 and a.layer == 1:
                    last.then_inc(core_done, 1)

            def quad(a, grp):
                pe.wait_ge(w_done, a.n(5, (2, 4, 5)[grp]))
                for pair in group(grp):
                    last = nc.tensor.matmul(out_of(pair), cst[0:M2[0], C_QSEL:C_QSEL + VW_COLS],
                                            wt[:, a.base % 2, pair, :], start=False, stop=True, skip_group_check=True)
                if grp == 2:
                    last.then_inc(core_done, 1)

            def vk(a, _):
                n = a.base % 2
                pe.wait_ge(cw_in[n], a.block(16, 16))
                if a.base in (0, B):
                    pe.wait_ge(rest_in, 16 * 12)
                bank = claim_bank(pe, "vk", a, 0)
                m = M2[a.layer]
                if a.layer == 0:
                    accumulate(ps[0:m, bank, 0:T + C], [(cw[:, n, e, 0:m], cw[:, n, e, m:m + T + C])
                                                        for e in range(KE)], vk_ps)
                else:
                    accumulate(ps[0:m, bank, 0:C], [(cw1[:, n, e, :], wv1[:, e, :]) for e in range(KE)], vk_ps)

            def vw(a, _):
                pe.wait_ge(vpb_made, a.n(1, 1))
                bank = claim_bank(pe, "vw", a, 0)
                accumulate(ps[0:Z1, bank, 0:C], [(vpb[:, a.base % 2, h, :], wop[:, h, :]) for h in range(2)], vw_ps)

            def ot(a, tile):
                pe.wait_ge(ot_sb, a.n(1, 1))
                bank = claim_bank(pe, "ot", a, tile)
                for grp in range(3):
                    p = 32 * len(group(grp))
                    last = nc.tensor.transpose(ps[:, bank, grp * 128:grp * 128 + p],
                                               ots[0:p, grp, tile * 128:(tile + 1) * 128], cst[0:p, C_ID:C_ID + p])
                last.then_inc(ot_ps, 1)

            def zt_(a, _):
                if a.layer == 0:
                    pe.wait_ge(ip_z, a.n(1, 1))
                pe.wait_ge(z_made, a.n(2, 2))
                bank = claim_bank(pe, "zt", a, 0)
                for tile in range(2):
                    for h, (lo, hi) in enumerate(((0, 128), (128, C + H * N_IP)) if a.layer == 0 else ((0, HC), (HC, C))):
                        last = nc.tensor.transpose(ps[0:hi - lo, bank, h * S + tile * 128:h * S + (tile + 1) * 128],
                                                   z[:, tile, lo:hi], ident)
                last.then_inc(zt_ps, 1)

            def y(a, _):
                pe.wait_ge(zt_sb, a.n(1, 1))
                if a.layer == 0:
                    pe.wait_ge(wz_made, a.n(1, 1))
                bank = claim_bank(pe, "y", a, 0)
                for mh in range(2):
                    cols = slice(mh * HC, (mh + 1) * HC)
                    if a.layer == 0:
                        ops = [(wo0[:, cols], zt[:, 0, :]), (wz[:, a.base % 2, cols], zt[0:Z1, 1, :])]
                    else:
                        ops = [(wo1[:, h, cols], zt[0:HC, h, :]) for h in range(2)]
                    accumulate(ps[0:HC, bank, mh * S:(mh + 1) * S], ops, y_ps if mh else None)

            def settle(t):
                n = number[[(w, t + d, k) for w, d, k in PE_STEP if w in FILLS and present(w, t + d)][0]]
                for f in order[n - 2:n]:
                    pe.wait_ge(*consumed(f, At(f[1])))

            run(PE_STEP, {"q": q, "sc": sc, "mt": mt_, "st": st, "u": u, "pv": pv, "quad": quad, "vk": vk, "vw": vw,
                          "ot": ot, "zt": zt_, "y": y}, settle, {-2: late_setup})(pe)

        @block.scalar
        def _(act):
            nc.scalar.preload_act_table_set("natural_log_exp_and_others")
            act.dma_start(ca[:, :, :], ctxT).then_inc(c_in, 16)
            act.dma_start(wk[0][:, :, :], WK[0]).then_inc(c_in, 16)

            def keep_keys(layer):
                for half in range(2):
                    for n in range(2):
                        act.wait_ge(setup_ps, (9 if layer else 0) + 2 * half + n + 1)
                        nc.scalar.copy(kt[layer][:, half, 8 * n:8 * n + 8, :],
                                       ps[0:HC, 2 + 2 * half + n, :].rearrange("p (b t) -> p b t", t=T)).then_inc(setup_sb, 1)

            keep_keys(0)
            act.wait_ge(setup_ps, 6)
            act.wait_ge(setup_sb, 4)
            for half in range(2):
                nc.scalar.copy(kt[0][:, half, :, T - N_IP:],
                               ps[0:HC, 6, half * 64:(half + 1) * 64].rearrange("p (b t) -> p b t", t=N_IP)).then_inc(setup_sb, 1)
            act.wait_ge(setup_ps, 9)
            nc.scalar.copy(vipt[:, :, :, :].rearrange("p h b t -> p (h b t)"), ps[0:HC, 7, 0:128]).then_inc(setup_sb, 1)
            nc.scalar.copy(inv[:, 0, :], ps[:, 7, 128:192]).then_inc(setup_sb, 1)
            act.wait_ge(inv_step, 1)
            nc.scalar.activation(inv[:, 1, :], inv[:, 0, :], ACT.Ln).then_inc(act_chain, 1)
            act.wait_ge(act_chain, 1)
            nc.scalar.activation(inv[:, 1, :], inv[:, 1, :], ACT.Exp, scale=-0.5).then_inc(inv_step, 1)

            def otev(a, _):
                act.wait_ge(core_done, a.n(1, 1))
                need(act, ot_ps, a.n(2, 0))
                nc.scalar.copy(ots[:, 0:2, :].rearrange("p a b -> p (a b)"), ps[:, 6, :])
                nc.scalar.copy(ots[0:64, 2, :], ps[0:64, 7, 0:S]).then_inc(ot_sb, 1)

            def qh(a, _):
                half = a.base % 2
                act.wait_ge(q_ps, a.n(1, 1))
                need(act, q_stacked[half], a.block(16 * len(Q_PARTS), 0))
                nc.scalar.copy(qp[:, 0, half, :], ps[0:HC, bank_of("q", a, 0), :]).then_inc(q_h, 1)

            def qm(a, _):
                act.wait_ge(q_r, a.n(1, 1))
                nc.scalar.copy(qp[:, 1, a.base % 2, :], qr[:, :]).then_inc(q_m, 1)

            def kh(a, _):
                act.wait_ge(k_mask, a.block(1, 1))
                need(act, k_stacked, a.block(32 * len(K_PARTS), 0))
                nc.scalar.copy(kp[:, 0, :, :, :].rearrange("p a b c -> p (a b c)"), kmk[:, :, :, :].rearrange("p a b c -> p (a b c)")).then_inc(k_h, 1)

            def km(a, _):
                act.wait_ge(k_r, a.block(1, 1))
                nc.scalar.copy(kp[:, 1, :, :, :].rearrange("p a b c -> p (a b c)"), krem[:, :, :, :].rearrange("p a b c -> p (a b c)")).then_inc(k_m, 1)

            def exp(a, c):
                m = M2[a.layer]
                act.wait_ge(st_ps, a.n(5, c + 1))
                if c == 0:
                    need(act, core_done, a.n(1, -1))
                nc.scalar.activation(pt[0:m, a.base % 2, 2 * c:2 * c + 2, :].rearrange("p a b -> p (a b)"),
                                     ps[0:m, 2 + (a.base + c) % 2, :], ACT.Exp, scale=SCALE).then_inc(exp_done, 1)

            def rsq(a, _):
                act.wait_ge(ip_q2, a.n(1, 1))
                nc.scalar.activation(e40[:, 2, :], e40[:, 1, :], ACT.Ln).then_inc(act_chain, 1)
                act.wait_ge(act_chain, a.n(1, 2))
                nc.scalar.activation(e40[:, 3, :], e40[:, 2, :], ACT.Exp, scale=-0.5).then_inc(ip_rsq, 1)

            def ipe(a, _):
                act.wait_ge(ip_less, a.n(1, 1))
                nc.scalar.activation(e160[:, 2, :, :], e160[:, 1, :, :], ACT.Exp).then_inc(ip_exp, 1)

            def mtev(a, _):
                act.wait_ge(mt_ps, a.n(1, 1))
                need(act, m_stacked[a.base % 2], a.block(32, 0))
                nc.scalar.copy(mt[:, a.base % 2, :], ps[0:8 * PAIRS, bank_of("mt", a, 0), 0:64].bitcast(BF16)).then_inc(mt_sb, 1)

            def ztev(a, _):
                act.wait_ge(zt_ps, a.n(1, 1))
                need(act, y_ps, a.n(1, 0))
                bank = bank_of("zt", a, 0)
                if a.layer == 0:
                    nc.scalar.copy(zt[:, 0, :], ps[:, bank, 0:S])
                    nc.scalar.copy(zt[0:Z1, 1, :], ps[0:Z1, bank, S:2 * S]).then_inc(zt_sb, 1)
                else:
                    nc.scalar.copy(zt[0:HC, :, :], ps[0:HC, bank, :].rearrange("p (a b) -> p a b", a=2)).then_inc(zt_sb, 1)

            run(ACT_STEP, {"otev": otev, "qh": qh, "qm": qm, "kh": kh, "km": km, "exp": exp, "rsq": rsq, "ipe": ipe,
                           "mtev": mtev, "ztev": ztev}, None, {-2: lambda: keep_keys(1)})(act)

        @block.vector
        def _(dve):
            for n in range(2):
                nc.vector.memset(vb[n][:, :, :, :], 0.0).then_inc(zeroed, 1)
            nc.vector.memset(vpb[:, :, :, 0:IP_ROW], 0.0).then_inc(zeroed, 1)
            dve.wait_ge(c_in, 32)
            ipc = ca[:, :, :].rearrange("p k (b t) -> p k b t", t=T)[:, :, :, T - N_IP:]
            for e in range(KE):
                last = nc.vector.tensor_tensor(ipsq[:, e, :].rearrange("p (b t) -> p b t", t=N_IP), ipc[:, e], ipc[:, e], ALU.mult)
            last.then_inc(sq_made, 1)
            dve.wait_ge(w_in, 32)
            dve.wait_ge(zeroed, 3)
            for n, col in ((0, C_MHH0), (1, C_MHH1)):
                for ring in range(2):
                    nc.vector.tensor_copy(vb[n][:, ring, :, SUM0:SUM0 + 2],
                                          cst[0:M2[n], col:col + 2].unsqueeze(1).broadcast_to([M2[n], PAIRS, 2])).then_inc(vsum, 1)

            def qr_(a, _):
                half = a.base % 2
                dve.wait_ge(q_h, a.n(1, 1))
                need(dve, q_l, a.n(1, 0))
                nc.vector.tensor_tensor(qr[:, :], ps[0:HC, bank_of("q", a, 0), :], qp[:, 0, half, :],
                                        ALU.subtract).then_inc(q_r, 1)

            def w(a, c):
                dve.wait_ge(u_ps, a.n(5, c + 1))
                if c == 0:
                    need(dve, core_done, a.n(1, -1))
                r = a.base % 2
                nc.vector.tensor_tensor(wt[:, r, 2 * c:2 * c + 2, :].rearrange("p a b -> p (a b)"),
                                        ps[0:M2[0], 4 + (a.base + c) % 2, :],
                                        pt[0:M2[0], r, 2 * c:2 * c + 2, :].rearrange("p a b -> p (a b)"),
                                        ALU.mult).then_inc(w_done, 1)

            def on(a, tile):
                dve.wait_ge(ot_ps, a.n(2, tile + 1))
                o = ps[:, bank_of("ot", a, tile), 0:PAIRS * VW_COLS].rearrange("p (a c) -> p a c", c=VW_COLS)
                if tile == 0:
                    need(dve, z_made, a.n(2, 0))
                nc.vector.reciprocal(rs[:, tile, :, :], o[:, :, SUM0:SUM0 + 2]).then_inc(r_made, 1)
                if a.layer == 0:
                    need(dve, ip_fused, a.n(1, 0))
                    nc.vector.tensor_copy(stat[:, tile, :, :], o[:, :, NUM0:NUM0 + 12]).then_inc(stat_made, 1)
                need(dve, zt_ps, a.n(1, 0))
                dve.wait_ge(r_made, a.n(2, tile + 1))
                nc.vector.tensor_tensor(z[:, tile, 0:C].rearrange("p (a b c) -> p a b c", b=2, c=D),
                                        o[:, :, 0:R].rearrange("p a (b c) -> p a b c", c=D),
                                        rs[:, tile, :, :].unsqueeze(3).broadcast_to([128, PAIRS, 2, D]),
                                        ALU.mult).then_inc(z_made, 1)

            def red(a, f):
                nt = NT[a.layer]
                dve.wait_ge(sc_ps, a.n(5, f + 1))
                if f == 0:
                    need(dve, m_lo, a.n(1, 0))
                parts = [(f // 2, 4 * (f % 2), 4, 0)] if f < 4 else [(0, 8, 2, 0), (1, 8, 2, 256)]
                for tile, p0, np_, c0 in parts:
                    o = ps[:, bank_of("sc", a, f), c0:c0 + np_ * 128].rearrange("p (a c) -> p a c", c=128)
                    if a.layer == 0:
                        nc.vector.tensor_copy(ipraw[:, a.base % 4, tile, p0:p0 + np_, :], o[:, :, M2[0]:128])
                    nc.vector.tensor_reduce(mx[:, tile, p0:p0 + np_, :],
                                            o[:, :, 0:2 * nt].rearrange("p a (h t) -> p a h t", t=nt),
                                            AX_X, ALU.max).then_inc(red_done, 1)

            def neg(a, _):
                dve.wait_ge(red_done, a.n(6, 6))
                need(dve, mt_ps, a.n(1, 0))
                src = mx[:, :, :, :].rearrange("p t a h -> p t h a")
                nc.vector.tensor_scalar(mc[:, :, 0, :, :], src, -1.0, None, ALU.mult).then_inc(m_hi, 1)
                dve.wait_ge(m_hi, a.n(1, 1))
                for tile in range(2):
                    last = nc.vector.scalar_tensor_tensor(mc[:, tile, 1, :, :], src[:, tile], -1.0, mc[:, tile, 0, :, :],
                                                          ALU.mult, ALU.subtract)
                last.then_inc(m_lo, 1)

            def ipa(a, _):
                dve.wait_ge(stat_made, a.n(2, 2))
                need(dve, ip_fused, a.n(1, 0))
                nc.vector.scalar_tensor_tensor(by_head(e40[:, 0, :]), stats(8, 10), EPS2, stats(8, 10),
                                               ALU.mult, ALU.mult).then_inc(ip_least, 1)
                dve.wait_ge(ip_least, a.n(1, 1))
                nc.vector.tensor_tensor(by_head(e40[:, 1, :]), by_head(e40[:, 0, :]), stats(10, 12),
                                        ALU.max).then_inc(ip_q2, 1)
                dve.wait_ge(ip_q2, a.n(1, 1))
                nc.vector.tensor_scalar(e40[:, 0, :], e40[:, 1, :], -0.5, None, ALU.mult).then_inc(ip_half, 1)

            def ipm(a, _):
                dve.wait_ge(ip_fused, a.n(1, 1))
                nc.vector.tensor_reduce(e40[:, 7, :], e160[:, 0, :, :], AX_X, ALU.max).then_inc(ip_max, 1)

            def ipr(a, _):
                dve.wait_ge(ip_exp, a.n(1, 1))
                nc.vector.tensor_reduce(e40[:, 5, :], e160[:, 2, :, :], AX_X, ALU.add).then_inc(ip_sum, 1)
                dve.wait_ge(ip_sum, a.n(1, 1))
                nc.vector.reciprocal(e40[:, 6, :], e40[:, 5, :]).then_inc(ip_rec, 1)

            def vprep(a, _):
                m, r, lay = M2[a.layer], a.base % 2, a.layer
                dve.wait_ge(vk_ps, a.n(1, 1))
                need(dve, core_done, a.n(1, -1))
                o = ps[0:m, bank_of("vk", a, 0), :]
                mv, v0 = (C_MV1, 0) if lay else (C_MV0, T)
                nc.vector.tensor_tensor(vb[lay][:, r, :, 0:R], o[:, v0:v0 + C].rearrange("p (a c) -> p a c", c=R),
                                        cst[0:m, mv:mv + R].unsqueeze(1).broadcast_to([m, PAIRS, R]),
                                        ALU.mult).then_inc(v_made, 1)
                if lay:
                    return
                if a.base == 0:
                    dve.wait_ge(simw_made, 1)
                need(dve, simv_made, a.n(1, 0))
                nc.vector.tensor_tensor(sim8[:, :, :], o[:, NT[0]:T].unsqueeze(1).broadcast_to([m, 2, N_IP]),
                                        simw[:, bass.ds(a.n(), 1), :, :].rearrange("p o h n -> p (o h) n"),
                                        ALU.mult).then_inc(sim_made, 1)
                nc.vector.tensor_tensor(gram[:, r, :].rearrange("p (h t) -> p h t", h=2),
                                        o[:, 0:NT[0]].unsqueeze(1).broadcast_to([m, 2, NT[0]]),
                                        cst[0:m, C_MHH0:C_MHH0 + 2].unsqueeze(2).broadcast_to([m, 2, NT[0]]),
                                        ALU.mult).then_inc(gram_made, 1)
                dve.wait_ge(sim_made, a.n(1, 1))
                nc.vector.tensor_copy(vb[0][:, r, :, NUM0:NUM0 + 8],
                                      sim8[:, :, :].rearrange("p a b -> p (a b)").unsqueeze(1).broadcast_to([m, PAIRS, 8])
                                      ).then_inc(simv_made, 1)

            def wz_(a, _):
                dve.wait_ge(vw_ps, a.n(1, 1))
                need(dve, y_ps, a.n(1, -1))
                nc.vector.tensor_tensor(wz[:, a.base % 2, :], ps[0:Z1, bank_of("vw", a, 0), 0:C], wrem[:, :],
                                        ALU.add).then_inc(wz_made, 1)

            def ysb(a, _):
                dve.wait_ge(y_ps, a.n(1, 1))
                bank = bank_of("y", a, 0)
                rows = bass.ds(a.n(S, -a.layer * ROWS), S)
                for mh in range(2):
                    last = nc.vector.scalar_tensor_tensor(x[:, mh, rows], ps[0:HC, bank, mh * S:(mh + 1) * S],
                                                          bo[:, a.layer, mh:mh + 1], x[:, mh, rows], ALU.add, ALU.add)
                last.then_inc(y_sb, 1)

            run(DVE_STEP, {"qr": qr_, "w": w, "on": on, "red": red, "neg": neg, "ipa": ipa, "ipm": ipm, "ipr": ipr, "vprep": vprep,
                           "wz": wz_, "ysb": ysb})(dve)

        @block.gpsimd
        def _(pool):
            tt = nc.gpsimd.tensor_tensor
            pool.wait_ge(setup_sb, 8)
            nc.gpsimd.tensor_scalar(inv[:, 0, :], inv[:, 0, :], EPS2, None, ALU.max).then_inc(inv_step, 1)
            pool.wait_ge(inv_step, 2)
            tt(inv[:, 2, :], inv[:, 1, :], inv[:, 1, :], ALU.mult).then_inc(inv_step, 1)
            pool.wait_ge(inv_step, 3)
            tt(inv[:, 2, :], inv[:, 2, :], inv[:, 0, :], ALU.mult).then_inc(inv_step, 1)
            pool.wait_ge(inv_step, 4)
            nc.gpsimd.tensor_scalar(inv[:, 2, :], inv[:, 2, :], -0.5 * SEM_SCALE, 1.5 * SEM_SCALE,
                                    ALU.mult, ALU.add).then_inc(inv_step, 1)
            pool.wait_ge(inv_step, 5)
            tt(inv[:, 3, :], inv[:, 2, :], inv[:, 1, :], ALU.mult).then_inc(inv_step, 1)
            pool.wait_ge(inv_step, 6)
            pool.wait_ge(w_in, 32)
            for hh in range(2):
                last = nc.gpsimd.tensor_scalar(simw[:, :, hh, :], inv[0:M2[0], 3, :].rearrange("p (b n) -> p b n", n=N_IP),
                                               cst[0:M2[0], C_MHH0 + hh:C_MHH0 + hh + 1], None, ALU.mult)
            last.then_inc(simw_made, 1)

            def kmask(a, _):
                lay, nt = a.layer, NT[a.layer]
                if a.base == 0:
                    pool.wait_ge(w_in, 32)
                    pool.wait_ge(setup_sb, 6)
                elif a.base == B:
                    pool.wait_ge(setup_sb, 12)
                need(pool, k_l, a.block(1, 0))
                bs = bass.ds(a.n(1, -lay * B), 2)
                mask = cst[0:HC, C_KHH:C_KHH + 2].unsqueeze(1).unsqueeze(3)
                for half in range(2):
                    out = kmk[:, half, :, :]
                    last = tt(out[:, :, 0:2 * nt].rearrange("p b (h t) -> p b h t", h=2),
                              kt[lay][:, half, bs, 0:nt].unsqueeze(2).broadcast_to([HC, 2, 2, nt]),
                              mask.broadcast_to([HC, 2, 2, nt]), ALU.mult)
                    if lay == 0:
                        last = tt(out[:, :, 2 * nt:].rearrange("p b (h t) -> p b h t", h=2),
                                  kt[0][:, half, bs, nt:T].unsqueeze(2).broadcast_to([HC, 2, 2, N_IP]),
                                  mask.broadcast_to([HC, 2, 2, N_IP]), ALU.mult)
                last.then_inc(k_mask, 1)

            def flat(ap):
                return ap.rearrange("p a b c -> p (a b c)")

            def kr(a, _):
                pool.wait_ge(k_h, a.block(1, 1))
                tt(flat(krem[:, :, :, :]), flat(kmk[:, :, :, :]), flat(kp[:, 0, :, :, :]), ALU.subtract).then_inc(k_r, 1)

            def kl(a, _):
                pool.wait_ge(k_m, a.block(1, 1))
                tt(flat(kp[:, 2, :, :, :]), flat(krem[:, :, :, :]), flat(kp[:, 1, :, :, :]), ALU.subtract).then_inc(k_l, 1)

            def ql(a, _):
                half = a.base % 2
                pool.wait_ge(q_m, a.n(1, 1))
                tt(qp[:, 2, half, :], qr[:, :], qp[:, 1, half, :], ALU.subtract).then_inc(q_l, 1)

            def linked(a, per, k, ins):
                ins.then_inc(pool_chain, 1)
                pool.wait_ge(pool_chain, a.n(per, k))

            IPC = 7

            def ipb(a, _):
                pool.wait_ge(ip_half, a.n(1, 1))
                pool.wait_ge(ip_rsq, a.n(1, 1))
                r, r2, r15 = e40[:, 3, :], e40[:, 4, :], e40[:, 2, :]
                raw = ipraw[:, a.base % 4, :, :, :].rearrange("p t a (h n) -> p (t a h) n", n=N_IP)
                ins = tt(r2, r, r, ALU.mult)
                nc.gpsimd.tensor_scalar(r15, r, 1.5, None, ALU.mult)
                nc.gpsimd.tensor_scalar(e160[:, 1, :, :], raw, SCALE, None, ALU.mult)
                linked(a, IPC, 1, ins)
                linked(a, IPC, 2, tt(r2, r2, e40[:, 0, :], ALU.mult))
                linked(a, IPC, 3, tt(r2, r2, r, ALU.mult))
                linked(a, IPC, 4, tt(r2, r2, r15, ALU.add))
                linked(a, IPC, 5, tt(e160[:, 0, :, :].rearrange("p (a h) n -> p a h n", h=2),
                                     stats(0, 8).rearrange("p a (h n) -> p a h n", h=2),
                                     by_head(r2).unsqueeze(3).broadcast_to([128, 2 * PAIRS, 2, N_IP]), ALU.mult))
                tt(e160[:, 0, :, :], e160[:, 0, :, :], e160[:, 1, :, :], ALU.add).then_inc(ip_fused, 1)

            def ipd(a, _):
                pool.wait_ge(ip_max, a.n(1, 1))
                tt(e160[:, 1, :, :], e160[:, 0, :, :], e40[:, 7, :].unsqueeze(2).broadcast_to([128, 2 * H, N_IP]),
                   ALU.subtract).then_inc(ip_less, 1)

            def ipz(a, _):
                pool.wait_ge(ip_rec, a.n(1, 1))
                if a.base == 0:
                    pool.wait_ge(rest_in, 16 * 12)
                share = e40[:, 6, :].rearrange("p (t h) -> p t h", t=2)
                linked(a, IPC, 6, tt(share, share, fside[:, :].unsqueeze(2).broadcast_to([128, 2, H]), ALU.mult))
                need(pool, zt_ps, a.n(1, 0))
                for tile in range(2):
                    ins = tt(z[:, tile, C:].rearrange("p (a n) -> p a n", n=N_IP), e160[:, 2, tile * H:(tile + 1) * H, :],
                             e40[:, 6, tile * H:(tile + 1) * H].unsqueeze(2).broadcast_to([128, H, N_IP]), ALU.mult)
                    if tile:
                        ins.then_inc(ip_z, 1)
                    else:
                        linked(a, IPC, 7, ins)

            def vpb_(a, _):
                if a.base == 0:
                    pool.wait_ge(zeroed, 3)
                need(pool, vw_ps, a.n(1, -1))
                for half in range(2):
                    last = tt(vpb[:, a.base % 2, half, IP_ROW:].rearrange("p (h n) -> p h n", n=N_IP),
                              vipt[:, half, bass.ds(a.n(), 1), :].broadcast_to([HC, H, N_IP]),
                              cst[0:HC, C_MVH + half * H:C_MVH + (half + 1) * H].unsqueeze(2).broadcast_to([HC, H, N_IP]),
                              ALU.mult)
                last.then_inc(vpb_made, 1)

            run(POOL_STEP, {"kmask": kmask, "kr": kr, "kl": kl, "ql": ql, "ipb": ipb, "ipd": ipd,
                            "ipz": ipz, "vpb": vpb_})(pool)


def kernel(x, ctx_2048, fside_S_0, L0_xattn_W_q, L0_xattn_W_k, L0_xattn_W_v, L0_xattn_W_k_ip, L0_xattn_W_v_ip,
           L0_xattn_W_out, L0_xattn_b_out, L1_xattn_Wq, L1_xattn_Wk, L1_xattn_Wv, L1_xattn_Wk_ip, L1_xattn_Wv_ip,
           L1_xattn_Wo, L1_xattn_bo):
    import concourse.bacc as bacc
    from concourse.bass_utils import run_bass_kernel_spmd

    def tiles(w, p):
        w = np.asarray(w)
        return w.reshape(-1, p, w.shape[1]).transpose(1, 0, 2)

    perm = np.arange(C).reshape(2, HP, R).transpose(0, 2, 1).ravel()
    wq0, wq1 = np.asarray(L0_xattn_W_q)[:, perm], np.asarray(L1_xattn_Wq).T[:, perm]
    wk0, wk1 = np.asarray(L0_xattn_W_k)[:, perm], np.asarray(L1_xattn_Wk).T[:, perm]
    ctx = np.asarray(ctx_2048).transpose(0, 2, 1).reshape(B, KE, 128, T).transpose(0, 2, 1, 3)
    text = ctx[..., :NT[0]]
    wo = np.asarray(L0_xattn_W_out)
    wrem = np.zeros((Z1, C), np.float32)
    wrem[:C - 128] = wo[128:]
    consts, ones_rows, ident16 = constants()
    data = {
        "xT": np.asarray(x).reshape(ROWS, 2, HC).transpose(2, 1, 0),
        "ctxT": ctx.transpose(1, 2, 0, 3).reshape(128, KE, B * T),
        "ctx0": np.concatenate([text, text, ctx], axis=3),
        "ctx1": np.concatenate([ctx, ctx], axis=3),
        "side": np.asarray(fside_S_0).reshape(2, 128).T,
        "WQ": np.stack([tiles(wq0, HC), tiles(wq1, HC)]),
        "WK": np.stack([tiles(wk0, 128), tiles(wk1, 128)]),
        "WKIP": tiles(np.asarray(L0_xattn_W_k_ip)[:, perm], 128),
        "WV": np.stack([tiles(L0_xattn_W_v, 128), tiles(np.asarray(L1_xattn_Wv).T, 128)]),
        "WVIP": tiles(L0_xattn_W_v_ip, 128),
        "WO0": wo[:128],
        "WREM": wrem,
        "WOP": tiles(wo, HC),
        "WO1": tiles(np.asarray(L1_xattn_Wo).T, HC),
        "BO": np.stack([np.asarray(L0_xattn_b_out).reshape(2, HC).T, np.asarray(L1_xattn_bo).reshape(2, HC).T], axis=1),
        "consts": consts,
        "ones_rows": ones_rows,
        "ident16": ident16,
    }
    nc = bacc.Bacc("TRN2", target_bir_lowering=False, num_devices=1)
    arrays, args = {}, {}
    for name, a in data.items():
        a = np.ascontiguousarray(a)
        arrays["in_" + name] = a
        args[name] = nc.dram_tensor("in_" + name, a.shape, mybir.dt.from_np(a.dtype), kind="ExternalInput").ap()
    args["outT"] = nc.dram_tensor("out_T", (HC, 2, ROWS), F32, kind="ExternalOutput").ap()
    xattn_kernel(nc, **args)
    result = run_bass_kernel_spmd(nc, [arrays], core_ids=[0]).results[0]["out_T"]
    return result.transpose(2, 1, 0).reshape(B, S, C)
```

```python
from contextlib import ExitStack

import numpy as np

import concourse.bass as bass
from concourse import mybir

F32 = mybir.dt.float32
BF16 = mybir.dt.bfloat16
ALU = mybir.AluOpType
ACT = mybir.ActivationFunctionType
AX_X = mybir.AxisListType.X

B, S, C, E, T = 16, 256, 160, 256, 64
H, D = 20, 8
N_IP = 4
PAIRS, R = H // 2, 2 * D
HC = C // 2
HP = PAIRS // 2
ROWS = B * S
NT = (T - N_IP, T)
M2 = (2 * NT[0], 2 * NT[1])
SCALE = float(D) ** -0.5
EPS2 = 1e-24
SEM_SCALE = 0.5

Q_PARTS = (0, 0, 0, 1, 1, 2)
K_PARTS = (0, 1, 2, 0, 1, 0)
KR = 16 * len(Q_PARTS)
KM = KR + 4
V_COLS, NUM0, SUM0, QUAD0, VW_COLS = 16, 16, 24, 26, 32
KE = 2
IP_ROW = 32
Z1 = IP_ROW + H * N_IP
STEPS_UNROLLED = 4
WARM_UP = 4
N_G = 2 * B

C_ID, C_KHH, C_MV0, C_MV1, C_MHH0, C_MHH1, C_QSEL, C_MVH, C_ONE, C_END = np.cumsum(
    [0, 128, 2, 16, 16, 2, 2, VW_COLS, 2 * H, 128]).tolist()


def constants():
    c = np.zeros((128, C_END), np.float32)
    c[:, C_ID:C_ID + 128] = np.eye(128)
    for p in range(HC):
        c[p, C_KHH + (p // HP) // D] = 1
    for layer, (mv, mhh) in enumerate(((C_MV0, C_MHH0), (C_MV1, C_MHH1))):
        for row in range(M2[layer]):
            hh = row // NT[layer]
            c[row, mv + hh * D:mv + hh * D + D] = 1
            c[row, mhh + hh] = 1
            if layer == 0:
                c[row, C_QSEL + QUAD0 + hh] = 1
    for half in range(2):
        for ch in range(HC):
            c[ch, C_MVH + half * H + (half * HC + ch) // D] = 1
    c[:, C_ONE:C_ONE + 128] = 1
    rows = np.zeros((2, 4, 128), np.float32)
    for layer in range(2):
        for part in range(2):
            for hh in range(2):
                rows[layer, 2 * part + hh, hh * NT[layer]:(hh + 1) * NT[layer]] = 1
    bf16 = mybir.dt.np(BF16)
    return c, rows.astype(bf16), np.eye(128).astype(bf16)


class At:

    def __init__(self, base, i=None):
        self.base, self.i = base, i

    def n(self, mul=1, add=0):
        v = self.base * mul + add
        return v if self.i is None else self.i * (STEPS_UNROLLED * mul) + v

    def block(self, mul=1, add=0):
        v = self.base // 2 * mul + add
        return v if self.i is None else self.i * (STEPS_UNROLLED // 2 * mul) + v

    def plus(self, k):
        return At(self.base + k, self.i)

    @property
    def layer(self):
        return self.base // B


def need(eng, sem, n):
    if not isinstance(n, int) or n > 0:
        eng.wait_ge(sem, n)


def fixed(eng, v):
    return v if isinstance(v, int) else eng.snap(v)


PE_STEP = [
    [("q", 3, 0), ("setup", 2, 0), ("keys1", 2, 0)],
    [("sc", 1, 0), ("sc", 1, 1), ("sc", 1, 2), ("sc", 1, 3), ("sc", 1, 4), ("vk", 1, 0), ("mt", 1, 0), ("q", 3, 0),
     ("q", 4, 0)],
    [("st", 0, 0), ("vk", 1, 0), ("st", 0, 1), ("ot", -1, 0), ("u", 0, 0), ("ot", -1, 1), ("sc", 1, 0),
     ("st", 0, 2), ("u", 0, 1), ("st", 0, 3), ("u", 0, 2), ("pv", 0, 0), ("sc", 1, 1), ("st", 0, 4), ("vw", -1, 0),
     ("u", 0, 3), ("zt", -2, 0), ("sc", 1, 2), ("sc", 1, 3), ("u", 0, 4), ("sc", 1, 4), ("quad", 0, 0),
     ("q", 4, 0), ("pv", 0, 1), ("mt", 1, 0), ("quad", 0, 1), ("pv", 0, 2), ("y", -2, 0)],
    [("sc", 1, 0), ("sc", 1, 1), ("st", 0, 0), ("sc", 1, 2), ("st", 0, 1), ("sc", 1, 3), ("ot", -1, 0),
     ("st", 0, 2), ("sc", 1, 4), ("pv", 0, 0), ("st", 0, 3), ("q", 4, 0), ("ot", -1, 1), ("zt", -2, 0),
     ("st", 0, 4), ("mt", 1, 0), ("pv", 0, 1), ("vw", -1, 0), ("vk", 1, 0), ("y", -2, 0), ("pv", 0, 2)]]
ACT_STEP = [
    [("qh", 3, 0), ("kh", 3, 0), ("qm", 3, 0), ("km", 3, 0), ("setup", 2, 0), ("iplen", 2, 0), ("keys1", 2, 0)],
    [("mtev", 1, 0), ("kh", 3, 0), ("qh", 3, 0), ("km", 3, 0), ("qm", 3, 0), ("qh", 4, 0), ("qm", 4, 0)],
    [("exp", 0, 0), ("exp", 0, 1), ("ipe", -2, 0), ("exp", 0, 2), ("exp", 0, 3), ("exp", 0, 4), ("ztev", -2, 0),
     ("rsq", -1, 0), ("kh", 3, 0), ("km", 3, 0), ("qh", 4, 0), ("mtev", 1, 0), ("qm", 4, 0), ("otev", 0, 0)],
    [("exp", 0, 0), ("exp", 0, 1), ("ipe", -2, 0), ("exp", 0, 2), ("exp", 0, 3), ("qh", 4, 0), ("exp", 0, 4),
     ("mtev", 1, 0), ("qm", 4, 0), ("ztev", -2, 0), ("kh", 3, 0), ("km", 3, 0), ("rsq", -1, 0), ("otev", 0, 0)]]
DVE_STEP = [
    [("qr", 3, 0), ("kr", 3, 0), ("ql", 3, 0), ("kmask", 4, 0), ("kl", 3, 0)],
    [("red", 1, 0), ("red", 1, 1), ("red", 1, 2), ("red", 1, 3), ("red", 1, 4), ("neg", 1, 0), ("vprep", 1, 0),
     ("kr", 3, 0), ("qr", 3, 0), ("kl", 3, 0), ("ql", 3, 0), ("qr", 4, 0), ("ql", 4, 0)],
    [("ipm", -2, 0), ("on", -1, 0), ("w", 0, 0), ("on", -1, 1), ("ipr", -2, 0), ("vprep", 1, 0), ("w", 0, 1),
     ("red", 1, 0), ("ipa", -1, 0), ("w", 0, 2), ("red", 1, 1), ("wz", -1, 0), ("w", 0, 3), ("red", 1, 2),
     ("red", 1, 3), ("w", 0, 4), ("red", 1, 4), ("neg", 1, 0), ("qr", 4, 0), ("ysb", -2, 0)],
    [("ipm", -2, 0), ("red", 1, 0), ("red", 1, 1), ("ipr", -2, 0), ("red", 1, 2), ("red", 1, 3), ("on", -1, 0),
     ("red", 1, 4), ("neg", 1, 0), ("on", -1, 1), ("qr", 4, 0), ("ipa", -1, 0), ("wz", -1, 0), ("vprep", 1, 0),
     ("ysb", -2, 0)]]
POOL_STEP = [
    [("iplen", 2, 0)],
    [],
    [("ipd", -2, 0), ("ipz", -2, 0), ("kr", 3, 0), ("ipb", -1, 0), ("vpb", 0, 0), ("kl", 3, 0), ("ql", 4, 0),
     ("kmask", 4, 0)],
    [("ipd", -2, 0), ("ipz", -2, 0), ("ql", 4, 0), ("kr", 3, 0), ("ipb", -1, 0), ("vpb", 0, 0), ("kl", 3, 0),
     ("kmask", 4, 0)]]
SP_STEP = [
    [("qd", 3, 0), ("cwd", 2, 0), ("kd", 3, 0)],
    [("cwd", 2, 0), ("mtd", 1, 0), ("qd", 4, 0), ("kd", 3, 0)],
    [("cwd", 2, 0), ("outd", -2, 0), ("mtd", 1, 0), ("qd", 4, 0), ("kd", 3, 0)],
    [("cwd", 2, 0), ("mtd", 1, 0), ("qd", 4, 0), ("kd", 3, 0), ("outd", -2, 0)]]
FILLS = ("q", "ot", "sc", "vk", "mt", "zt", "vw", "y")
SMALL_FILLS, SMALL0 = ("vk", "vw"), 256
SHARED_BANKS = ((0, 1), (0, 1, 4, 5))
LAYER0_ONLY = ("u", "quad", "vw", "w", "wz", "rsq", "ipe", "ipr", "ipa", "ipb", "ipm", "ipd", "vpb", "ipz")
LAYER1_ONLY = ("outd",)
BY_BLOCK = ("kh", "km", "kmask", "kr", "kl", "kd")
ONCE = ("setup", "iplen", "keys1")
FIRST_STEP, LAST_STEP = -4, N_G + 1
LOOPS = {4: 2, B + 2: 2}


def present(what, g):
    if not 0 <= g < N_G or (what in BY_BLOCK and g % 2) or (what == "qd" and g % 2 == 0) or (what in ONCE and g):
        return False
    return not ((what in LAYER0_ONLY and g >= B) or (what in LAYER1_ONLY and g < B))


def stages_of(steps, t):
    return [(w, d, k) for w, d, k in steps[(t >= -1) + (t >= 0) + (t >= B)] if present(w, t + d)]


def bank_users():
    order, plan, last, turn = [], {}, {}, 0
    for t in range(FIRST_STEP, LAST_STEP + 1):
        banks = SHARED_BANKS[t >= B]
        for w, d, k in stages_of(PE_STEP, t):
            if w in SMALL_FILLS or (w, k) == ("pv", 2):
                bank = 7
            elif w in FILLS:
                bank, turn = banks[turn % len(banks)], turn + 1
            elif w == "u":
                bank = 4 + (t + d + k) % 2
            else:
                continue
            f = (w, t + d, k)
            order.append((t, f))
            plan[f] = bank, last.get(bank)
            last[bank] = f
    return order, plan


def xattn_kernel(nc, xT, ctxT, ctx0, ctx1, side, WQ, WK, WKIP, WV, WVIP, WO0, WREM, WOP, WO1, BO,
                 consts, ones_rows, ident16, outT):
    order, plan = bank_users()

    with ExitStack() as stack:
        def sb(name, shape, dt=F32):
            return stack.enter_context(nc.sbuf_tensor(name, shape, dt))

        def sem(name):
            return stack.enter_context(nc.semaphore(name))

        cst = sb("cst", [128, C_END])
        id16 = sb("id16", [128, 128], BF16)
        wq = [sb(f"wq{n}", [HC, 2, C]) for n in range(2)]
        wk = [sb(f"wk{n}", [128, KE, C]) for n in range(2)]
        wkip, wvip = sb("wkip", [128, KE, C]), sb("wvip", [128, KE, C])
        wv1 = sb("wv1", [128, KE, C])
        wo0 = sb("wo0", [128, C])
        wrem = sb("wrem", [Z1, C])
        wop = sb("wop", [HC, 2, C])
        wo1 = sb("wo1", [HC, 2, C])
        bo = sb("bo", [HC, 2, 2])
        fside = sb("fside", [128, 2])
        x = sb("x", [HC, 2, ROWS])
        ca = sb("ca", [128, KE, B * T])
        kt = [sb(f"kt{n}", [HC, 2, B, T]) for n in range(2)]
        vipt = sb("vipt", [HC, 2, B, N_IP])
        ipsq = sb("ipsq", [128, KE, B * N_IP])
        inv = sb("inv", [128, 4, B * N_IP])
        simw = sb("simw", [M2[0], B, 2, N_IP])
        qp = sb("qp", [HC, 3, 2, 2 * S], BF16)
        qr = sb("qr", [HC, 2 * S])
        kmk = sb("kmk", [HC, 2, 2, 128])
        kp = sb("kp", [HC, 3, 2, 2, 128], BF16)
        krem = sb("krem", [HC, 2, 2, 128])
        qs = sb("qs", [128, 2, PAIRS, 2 * S], BF16)
        ks = [sb(f"ks{n}", [128, 2, PAIRS, 2, 128], BF16) for n in range(2)]
        mx = sb("mx", [128, 2, PAIRS, 2])
        mc = sb("mc", [128, 2, 2, 2, PAIRS], BF16)
        mt = sb("mt", [4 * PAIRS, 2, S], BF16)
        ipraw = sb("ipraw", [128, 4, 2, PAIRS, 2 * N_IP])
        pt = sb("pt", [128, 2, PAIRS, S])
        wt = sb("wt", [M2[0], 2, PAIRS, S])
        vb = [sb(f"vb{n}", [M2[n], 2, PAIRS, VW_COLS]) for n in range(2)]
        sim8 = sb("sim8", [M2[0], 2, N_IP])
        gram = sb("gram", [M2[0], 2, M2[0]])
        cw = sb("cw", [128, 2, KE, M2[0] + T + C])
        cw1 = sb("cw1", [128, 2, KE, M2[1]])
        vpb = sb("vpb", [HC, 2, 2, Z1])
        wz = sb("wz", [Z1, 2, C])
        ots = sb("ots", [128, 3, S])
        rs = sb("rs", [128, 2, PAIRS, 2])
        stat = sb("stat", [128, 2, PAIRS, 12])
        z = sb("z", [128, 2, 2, C + H * N_IP])
        zt = sb("zt", [128, 2, S])
        e40 = sb("e40", [128, 8, 2 * H])
        e160 = sb("e160", [128, 3, 2 * H, N_IP])

        ps = stack.enter_context(nc.psum_tensor("ps", [128, 8, 512], F32))

        w_in, rest_in = sem("w_in"), sem("rest_in")
        c_in, kv_in = [sem(f"c_in{n}") for n in range(2)], [sem(f"kv_in{n}") for n in range(2)]
        x_in = [sem(f"x_in{n}") for n in range(3)]
        rows_in = sem("rows_in")
        wt_zeroed, zeroed, vsum, sq_made = sem("wt_zeroed"), sem("zeroed"), sem("vsum"), sem("sq_made")
        setup_ps, setup_sb, inv_step, simw_made = sem("setup_ps"), sem("setup_sb"), sem("inv_step"), sem("simw_made")
        q_ps, q_h, q_r, q_m, q_l = (sem(f"q_{n}") for n in ("ps", "h", "r", "m", "l"))
        k_mask, k_h, k_r, k_m, k_l = (sem(f"k_{n}") for n in ("mask", "h", "r", "m", "l"))
        q_stacked, k_stacked = sem("q_stacked"), sem("k_stacked")
        m_stacked = [sem(f"m_stacked{n}") for n in range(2)]
        cw_in = [sem(f"cw_in{n}") for n in range(2)]
        sc_ps, red_done, m_hi, m_lo, mt_ps, mt_sb = (
            sem(n) for n in ("sc_ps", "red_done", "m_hi", "m_lo", "mt_ps", "mt_sb"))
        st_ps, exp_done, u_ps, w_done, core_done = (sem(n) for n in ("st_ps", "exp_done", "u_ps", "w_done", "core_done"))
        vk_ps, v_made, sim_made, gram_made, simv_made = (
            sem(n) for n in ("vk_ps", "v_made", "sim_made", "gram_made", "simv_made"))
        vpb_made, vw_ps, wz_made = sem("vpb_made"), sem("vw_ps"), sem("wz_made")
        ot_sb, ot_ps, r_made, stat_made, z_made = (sem(n) for n in ("ot_sb", "ot_ps", "r_made", "stat_made", "z_made"))
        ip_least, ip_q2, ip_half, ip_rsq, ip_fused, ip_max, ip_less, ip_exp, ip_sum, ip_rec, ip_z = (
            sem(n) for n in ("ip_least", "ip_q2", "ip_half", "ip_rsq", "ip_fused", "ip_max", "ip_less", "ip_exp", "ip_sum",
                             "ip_rec", "ip_z"))
        pool_chain, act_chain = sem("pool_chain"), sem("act_chain")
        zt_ps, zt_sb, y_ps, y_sb, out_done = (sem(n) for n in ("zt_ps", "zt_sb", "y_ps", "y_sb", "out_done"))

        ident = cst[:, C_ID:C_ID + 128]

        def stats(lo, hi):
            return stat[:, :, :, lo:hi].rearrange("p t a c -> p (t a) c")

        def last_group(a):
            return 128 if a.layer == 0 else 64

        def by_head(ap):
            return ap.rearrange("p (a h) -> p a h", h=2)

        def consumed(f, a):
            what, k = f[0], f[2]
            if what == "pv":
                return ot_sb, a.n(1, 1)
            if what == "u":
                return w_done, a.n(5, k + 1)
            if what == "q":
                return q_r, a.n(1, 1)
            if what == "ot":
                return z_made, a.n(2, k + 1)
            if what == "sc":
                return red_done, a.n(6, 6 if k == 4 else k + 1)
            if what == "vk":
                return (gram_made if a.layer == 0 else v_made), a.n(1, 1)
            return {"mt": mt_sb, "zt": zt_sb, "vw": wz_made, "y": y_sb}[what], a.n(1, 1)

        def bank_of(what, a, k):
            return plan[what, a.base, k][0]

        def claim_bank(pe, what, a, k):
            if a.i is None:
                bank, before = plan[what, a.base, k]
                if before:
                    pe.wait_ge(*consumed(before, At(before[1])))
                return bank
            bank, before = plan[what, a.base + STEPS_UNROLLED, k]
            pe.wait_ge(*consumed(before, At(before[1] - STEPS_UNROLLED, a.i)))
            assert bank == plan[what, a.base, k][0]
            return bank

        def run(steps, stages, before_loop=None):
            def body(t):
                for what, d, k in stages_of(steps, t.base):
                    stages[what](t.plus(d), k)

            def program(eng):
                t = FIRST_STEP
                while t <= LAST_STEP:
                    if t in LOOPS:
                        if before_loop:
                            before_loop(t)
                        with eng.Fori(0, LOOPS[t]) as i:
                            for u in range(STEPS_UNROLLED):
                                body(At(t + u, i))
                        t += STEPS_UNROLLED * LOOPS[t]
                    else:
                        body(At(t))
                        t += 1
            return program

        def splits(eng, tt):
            def kmask(a, _):
                lay, nt = a.layer, NT[a.layer]
                if a.base == 0:
                    eng.wait_ge(w_in, 32)
                    eng.wait_ge(setup_sb, 4)
                elif a.base == 2:
                    eng.wait_ge(setup_sb, 6)
                elif a.base == B:
                    eng.wait_ge(setup_sb, 12)
                need(eng, k_l, a.block(1, 0))
                bs = bass.ds(a.n(1, -lay * B), 2)
                mask = cst[0:HC, C_KHH:C_KHH + 2].unsqueeze(1).unsqueeze(3)
                for half in range(2):
                    out = kmk[:, half, :, :]
                    last = tt(out[:, :, 0:2 * nt].rearrange("p b (h t) -> p b h t", h=2),
                              kt[lay][:, half, bs, 0:nt].unsqueeze(2).broadcast_to([HC, 2, 2, nt]),
                              mask.broadcast_to([HC, 2, 2, nt]), ALU.mult)
                    if lay == 0:
                        last = tt(out[:, :, 2 * nt:].rearrange("p b (h t) -> p b h t", h=2),
                                  kt[0][:, half, bs, nt:T].unsqueeze(2).broadcast_to([HC, 2, 2, N_IP]),
                                  mask.broadcast_to([HC, 2, 2, N_IP]), ALU.mult)
                last.then_inc(k_mask, 1)

            def flat(ap):
                return ap.rearrange("p a b c -> p (a b c)")

            def kr(a, _):
                eng.wait_ge(k_h, a.block(1, 1))
                tt(flat(krem[:, :, :, :]), flat(kmk[:, :, :, :]), flat(kp[:, 0, :, :, :]), ALU.subtract).then_inc(k_r, 1)

            def kl(a, _):
                eng.wait_ge(k_m, a.block(1, 1))
                tt(flat(kp[:, 2, :, :, :]), flat(krem[:, :, :, :]), flat(kp[:, 1, :, :, :]), ALU.subtract).then_inc(k_l, 1)

            def ql(a, _):
                half = a.base % 2
                eng.wait_ge(q_m, a.n(1, 1))
                tt(qp[:, 2, half, :], qr[:, :], qp[:, 1, half, :], ALU.subtract).then_inc(q_l, 1)

            return {"kmask": kmask, "kr": kr, "kl": kl, "ql": ql}

        block = stack.enter_context(nc.Block())

        @block.sync
        def _(sp):
            sp.dma_start(wk[0][:, :, :], WK[0]).then_inc(c_in[0], 16)
            sp.dma_start(wkip[:, :, :], WKIP).then_inc(kv_in[0], 16)
            sp.dma_start(x[:, :, 0:2 * S], xT[:, :, 0:2 * S]).then_inc(x_in[0], 16)
            sp.dma_start(wq[0][:, :, :], WQ[0]).then_inc(w_in, 16)
            sp.dma_start(cst[:, :], consts).then_inc(w_in, 16)
            sp.dma_start(wvip[:, :, :], WVIP).then_inc(kv_in[1], 16)
            for n in range(2):
                for slot in range(2):
                    for b2 in range(2):
                        sp.dma_start(ks[n][KR:KM, slot, :, b2, :],
                                     ones_rows[n].unsqueeze(1).broadcast_to([4, PAIRS, 128])).then_inc(rows_in, 16)
            for n in range(2):
                sp.dma_start(cw[:, n, :, M2[0] + T:], WV[0]).then_inc(rest_in, 16)
            sp.dma_start(id16[:, :], ident16).then_inc(rest_in, 16)
            sp.dma_start(x[:, :, 2 * S:4 * S], xT[:, :, 2 * S:4 * S]).then_inc(x_in[1], 16)
            sp.dma_start(wk[1][:, :, :], WK[1]).then_inc(rest_in, 16)
            sp.dma_start(wop[:, :, :], WOP).then_inc(rest_in, 16)
            sp.dma_start(wrem[:, :], WREM).then_inc(rest_in, 16)
            sp.dma_start(fside[:, :], side).then_inc(rest_in, 16)
            sp.dma_start(wo0[:, :], WO0).then_inc(rest_in, 16)
            sp.dma_start(bo[:, :, :], BO).then_inc(rest_in, 16)
            sp.dma_start(wq[1][:, :, :], WQ[1]).then_inc(rest_in, 16)
            sp.dma_start(wo1[:, :, :], WO1).then_inc(rest_in, 16)
            sp.dma_start(wv1[:, :, :], WV[1]).then_inc(rest_in, 16)
            sp.dma_start(x[:, :, 4 * S:], xT[:, :, 4 * S:]).then_inc(x_in[2], 16)

            def load_context(a, _):
                n = a.base % 2
                dst, src, first = ((cw[:, n, :, 0:M2[0] + T], ctx0, 0) if a.layer == 0
                                   else (cw1[:, n, :, :], ctx1, B))
                batch = fixed(sp, a.n(1, -first))
                need(sp, vk_ps, a.n(1, -1))
                sp.dma_start(dst, src[bass.ds(batch, 1)].rearrange("o p k t -> (o p) k t")).then_inc(cw_in[n], 16)

            def store(a, _):
                c = fixed(sp, a.n(S, -ROWS))
                sp.wait_ge(y_sb, a.n(1, 1))
                sp.dma_start(outT[:, :, bass.ds(c, S)], x[:, :, bass.ds(c, S)]).then_inc(out_done, 16)

            def stack_keys(a, _):
                slot = a.base // 2 % 2
                for part, made in enumerate((k_h, k_m, k_l)):
                    sp.wait_ge(made, a.block(1, 1))
                    for j in [j for j, p in enumerate(K_PARTS) if p == part]:
                        sp.dma_start(ks[a.layer][16 * j:16 * j + 16, slot, :, :, :], kp[:, part]).then_inc(k_stacked, 16)

            def stack_queries(a, _):
                slot = a.base // 2 % 2
                for part, made in enumerate((q_h, q_m, q_l)):
                    sp.wait_ge(made, a.n(1, 1))
                    for j in [j for j, p in enumerate(Q_PARTS) if p == part]:
                        sp.dma_start(qs[16 * j:16 * j + 16, slot, :, :], qp[:, part]).then_inc(q_stacked, 16)

            def stack_maxima(a, _):
                sp.wait_ge(mt_sb, a.n(1, 1))
                slot, b2 = a.base // 2 % 2, a.base % 2
                sp.dma_start(qs[KR:KM, slot, :, b2 * S:(b2 + 1) * S], mt[:, b2, :]).then_inc(m_stacked[b2], 16)

            run(SP_STEP, {"cwd": load_context, "outd": store, "kd": stack_keys, "qd": stack_queries,
                          "mtd": stack_maxima})(sp)
            sp.wait_ge(out_done, 16 * B)

        @block.tensor
        def _(pe):
            def accumulate(out, pairs_, sem_=None, **kw):
                for n, (l, r) in enumerate(pairs_):
                    last = nc.tensor.matmul(out, l, r, start=(n == 0), stop=(n == len(pairs_) - 1), **kw)
                if sem_ is not None:
                    last.then_inc(sem_, 1)

            def project_keys(layer, n):
                for half in range(2):
                    accumulate(ps[0:HC, 2 + 2 * half + n, :],
                               [(wk[layer][:, e, half * HC:(half + 1) * HC], ca[:, e, n * 512:(n + 1) * 512])
                                for e in range(KE)], setup_ps)

            ipc = ca[:, :, :].rearrange("p k (b t) -> p k b t", t=T)[:, :, :, T - N_IP:]

            def project_prompts(w, bank):
                for half in range(2):
                    accumulate(ps[0:HC, bank, half * 64:(half + 1) * 64],
                               [(w[:, e, half * HC:(half + 1) * HC], ipc[:, e]) for e in range(KE)], setup_ps)

            pe.wait_ge(wt_zeroed, 1)
            for _ in range(WARM_UP):
                nc.tensor.matmul(ps[:, 0, 0:S], wt[:, 0, 0, 0:128], wt[:, 0, 1, :], start=True, stop=True)
            pe.wait_ge(c_in[0], 32)
            project_keys(0, 0)
            pe.wait_ge(c_in[1], 16)
            pe.wait_ge(kv_in[0], 16)
            project_prompts(wkip, 6)

            def setup(a, _):
                project_keys(0, 1)
                pe.wait_ge(kv_in[1], 16)
                project_prompts(wvip, 7)
                pe.wait_ge(w_in, 32)
                pe.wait_ge(sq_made, 1)
                accumulate(ps[0:128, 7, 128:192], [(cst[:, C_ONE:C_ONE + 128], ipsq[:, e, :]) for e in range(KE)],
                           setup_ps)

            def keys1(a, _):
                pe.wait_ge(setup_sb, 8)
                pe.wait_ge(rest_in, 16 * 12)
                for n in range(2):
                    project_keys(1, n)

            def q(a, _):
                half, lay = a.base % 2, a.layer
                if lay == 0:
                    if a.base == 0:
                        pe.wait_ge(w_in, 32)
                        pe.wait_ge(x_in[0], 16)
                    elif a.base == 2:
                        pe.wait_ge(x_in[1], 16)
                    elif a.base == 4:
                        pe.wait_ge(x_in[2], 16)
                else:
                    pe.wait_ge(y_sb, a.block(2, 2 - B))
                bank = claim_bank(pe, "q", a, 0)
                rows = bass.ds(a.block(2 * S, -lay * ROWS), 2 * S)
                accumulate(ps[0:HC, bank, :], [(wq[lay][:, h, half * HC:(half + 1) * HC], x[:, h, rows])
                                               for h in range(2)], q_ps)

            def sc(a, f):
                slot, b2 = a.base // 2 % 2, a.base % 2
                if f == 0:
                    pe.wait_ge(q_stacked, a.block(16 * len(Q_PARTS), 16 * len(Q_PARTS)))
                    pe.wait_ge(k_stacked, a.block(16 * len(K_PARTS), 16 * len(K_PARTS)))
                bank = claim_bank(pe, "sc", a, f)
                units = [(f // 2, 4 * (f % 2) + n) for n in range(4)] if f < 4 else [(n // 2, 8 + n % 2) for n in range(4)]
                for n, (tile, pair) in enumerate(units):
                    c = b2 * S + tile * 128
                    last = nc.tensor.matmul(ps[:, bank, n * 128:(n + 1) * 128], qs[0:KR, slot, pair, c:c + 128],
                                            ks[a.layer][0:KR, slot, pair, b2, :], start=True, stop=True)
                last.then_inc(sc_ps, 1)

            def mt_(a, _):
                pe.wait_ge(m_lo, a.n(1, 1))
                if a.base == 0:
                    pe.wait_ge(rest_in, 16 * 12)
                bank = claim_bank(pe, "mt", a, 0)
                for tile in range(2):
                    last = nc.tensor.matmul(ps[0:4 * PAIRS, bank, tile * 128:(tile + 1) * 128],
                                            mc[:, tile].rearrange("p a b c -> p (a b c)"), id16[:, :], start=True, stop=True)
                last.then_inc(mt_ps, 1)

            def st(a, c):
                slot, b2, m = a.base // 2 % 2, a.base % 2, M2[a.layer]
                if c == 0:
                    pe.wait_ge(m_stacked[b2], a.block(16, 16))
                    if a.base in (0, B):
                        pe.wait_ge(rows_in, 16 * 8)
                if a.base == 0 and c == 0:
                    pe.wait_ge(setup_sb, 12)
                need(pe, exp_done, a.n(5, c - 1))
                for n in range(2):
                    pair = 2 * c + n
                    last = nc.tensor.matmul(ps[0:m, 2 + (a.base + c) % 2, n * S:(n + 1) * S],
                                            ks[a.layer][0:KM, slot, pair, b2, 0:m],
                                            qs[0:KM, slot, pair, b2 * S:(b2 + 1) * S], start=True, stop=True)
                last.then_inc(st_ps, 1)

            def u(a, c):
                if c == 0:
                    pe.wait_ge(gram_made, a.n(1, 1))
                pe.wait_ge(exp_done, a.n(5, c + 1))
                need(pe, w_done, a.n(5, c - 1))
                nc.tensor.matmul(ps[0:M2[0], 4 + (a.base + c) % 2, :], gram[:, a.base % 2, :],
                                 pt[0:M2[0], a.base % 2, 2 * c:2 * c + 2, :].rearrange("p a b -> p (a b)"),
                                 start=True, stop=True).then_inc(u_ps, 1)

            def out_of(pair):
                j, grp = pair % 4, pair // 4
                return ps[32 * j:32 * j + VW_COLS, 6 + grp // 2, (grp % 2) * S:(grp % 2 + 1) * S]

            def group(grp):
                return range(4 * grp, min(4 * grp + 4, PAIRS))

            def pv(a, grp):
                if grp == 0:
                    need(pe, ot_sb, a.n(1, 0))
                    if a.base == 0:
                        pe.wait_ge(setup_sb, 12)
                    pe.wait_ge(v_made if a.layer else simv_made, a.n(1, 1))
                    if a.base in (0, B):
                        pe.wait_ge(vsum, 4)
                pe.wait_ge(exp_done, a.n(5, (2, 4, 5)[grp]))
                if grp == 2:
                    claim_bank(pe, "pv", a, grp)
                m = M2[a.layer]
                if grp == 2 and a.layer == 0:
                    pe.wait_ge(w_done, a.n(5, 5))
                for pair in group(grp):
                    last = nc.tensor.matmul(out_of(pair), vb[a.layer][:, a.base % 2, pair, :],
                                            pt[0:m, a.base % 2, pair, :], start=(grp != 1),
                                            stop=(a.layer == 1 or grp == 2), skip_group_check=True)
                if grp == 2 and a.layer == 0:
                    for pair in group(grp):
                        last = nc.tensor.matmul(out_of(pair + 2), cst[0:M2[0], C_QSEL:C_QSEL + VW_COLS],
                                                wt[:, a.base % 2, pair, :], start=True, stop=True, skip_group_check=True)
                if grp == 2:
                    last.then_inc(core_done, 1)

            def quad(a, grp):
                pe.wait_ge(w_done, a.n(5, (2, 4)[grp]))
                for pair in group(grp):
                    nc.tensor.matmul(out_of(pair), cst[0:M2[0], C_QSEL:C_QSEL + VW_COLS],
                                     wt[:, a.base % 2, pair, :], start=False, stop=True, skip_group_check=True)

            def vk(a, _):
                n = a.base % 2
                pe.wait_ge(cw_in[n], a.block(16, 16))
                if a.base in (0, B):
                    pe.wait_ge(rest_in, 16 * 12)
                if a.base == 0:
                    pe.wait_ge(setup_sb, 8)
                bank = claim_bank(pe, "vk", a, 0)
                m = M2[a.layer]
                if a.layer == 0:
                    accumulate(ps[0:m, bank, SMALL0:SMALL0 + T + C], [(cw[:, n, e, 0:m], cw[:, n, e, m:m + T + C])
                                                        for e in range(KE)], vk_ps)
                else:
                    accumulate(ps[0:m, bank, SMALL0:SMALL0 + C], [(cw1[:, n, e, :], wv1[:, e, :]) for e in range(KE)], vk_ps)

            def vw(a, _):
                pe.wait_ge(vpb_made, a.n(1, 1))
                bank = claim_bank(pe, "vw", a, 0)
                accumulate(ps[0:Z1, bank, SMALL0:SMALL0 + C], [(vpb[:, a.base % 2, h, :], wop[:, h, :]) for h in range(2)], vw_ps)

            def ot(a, tile):
                pe.wait_ge(ot_sb, a.n(1, 1))
                bank = claim_bank(pe, "ot", a, tile)
                for grp in range(3):
                    p = last_group(a) if grp == 2 else 128
                    last = nc.tensor.transpose(ps[:, bank, grp * 128:grp * 128 + p],
                                               ots[0:p, grp, tile * 128:(tile + 1) * 128], cst[0:p, C_ID:C_ID + p])
                last.then_inc(ot_ps, 1)

            def zt_(a, _):
                if a.layer == 0:
                    pe.wait_ge(ip_z, a.n(1, 1))
                pe.wait_ge(z_made, a.n(2, 2))
                bank = claim_bank(pe, "zt", a, 0)
                for tile in range(2):
                    for h, (lo, hi) in enumerate(((0, 128), (128, C + H * N_IP)) if a.layer == 0 else ((0, HC), (HC, C))):
                        last = nc.tensor.transpose(ps[0:hi - lo, bank, h * S + tile * 128:h * S + (tile + 1) * 128],
                                                   z[:, a.base % 2, tile, lo:hi], ident)
                last.then_inc(zt_ps, 1)

            def y(a, _):
                pe.wait_ge(zt_sb, a.n(1, 1))
                if a.layer == 0:
                    pe.wait_ge(wz_made, a.n(1, 1))
                bank = claim_bank(pe, "y", a, 0)
                for mh in range(2):
                    cols = slice(mh * HC, (mh + 1) * HC)
                    if a.layer == 0:
                        ops = [(wo0[:, cols], zt[:, 0, :]), (wz[:, a.base % 2, cols], zt[0:Z1, 1, :])]
                    else:
                        ops = [(wo1[:, h, cols], zt[0:HC, h, :]) for h in range(2)]
                    accumulate(ps[0:HC, bank, mh * S:(mh + 1) * S], ops, y_ps if mh else None)

            def settle(t):
                last = {plan[f][0]: f for step, f in order if step < t}
                for bank in SHARED_BANKS[t >= B] + (7,):
                    pe.wait_ge(*consumed(last[bank], At(last[bank][1])))

            run(PE_STEP, {"q": q, "sc": sc, "mt": mt_, "st": st, "u": u, "pv": pv, "quad": quad, "vk": vk, "vw": vw,
                          "ot": ot, "zt": zt_, "y": y, "setup": setup, "keys1": keys1}, settle)(pe)

        @block.scalar
        def _(act):
            nc.scalar.preload_act_table_set("natural_log_exp_and_others")
            for n in range(2):
                cols = slice(n * 8 * T, (n + 1) * 8 * T)
                act.dma_start(ca[:, :, cols], ctxT[:, :, cols]).then_inc(c_in[n], 16)

            def keep_keys(layer, n, first):
                for half in range(2):
                    act.wait_ge(setup_ps, first + half)
                    nc.scalar.copy(kt[layer][:, half, 8 * n:8 * n + 8, 0:NT[layer]],
                                   ps[0:HC, 2 + 2 * half + n, :].rearrange("p (b t) -> p b t", t=T)[:, :, 0:NT[layer]]
                                   ).then_inc(setup_sb, 1)

            keep_keys(0, 0, 1)
            act.wait_ge(setup_ps, 4)
            for half in range(2):
                nc.scalar.copy(kt[0][:, half, :, T - N_IP:],
                               ps[0:HC, 6, half * 64:(half + 1) * 64].rearrange("p (b t) -> p b t", t=N_IP)).then_inc(setup_sb, 1)

            def setup(a, _):
                keep_keys(0, 1, 5)
                act.wait_ge(setup_ps, 9)
                nc.scalar.copy(vipt[:, :, :, :].rearrange("p h b t -> p (h b t)"), ps[0:HC, 7, 0:128]).then_inc(setup_sb, 1)
                nc.scalar.copy(inv[:, 0, :], ps[:, 7, 128:192]).then_inc(setup_sb, 1)

            def iplen(a, _):
                act.wait_ge(inv_step, 1)
                nc.scalar.activation(inv[:, 1, :], inv[:, 0, :], ACT.Ln).then_inc(act_chain, 1)
                act.wait_ge(act_chain, 1)
                nc.scalar.activation(inv[:, 1, :], inv[:, 1, :], ACT.Exp, scale=-0.5).then_inc(inv_step, 1)

            def keys1(a, _):
                for n in range(2):
                    keep_keys(1, n, 10 + 2 * n)

            def otev(a, _):
                act.wait_ge(core_done, a.n(1, 1))
                need(act, ot_ps, a.n(2, 0))
                nc.scalar.copy(ots[:, 0:2, :].rearrange("p a b -> p (a b)"), ps[:, 6, :])
                p = last_group(a)
                nc.scalar.copy(ots[0:p, 2, :], ps[0:p, 7, 0:S]).then_inc(ot_sb, 1)

            def qh(a, _):
                half = a.base % 2
                act.wait_ge(q_ps, a.n(1, 1))
                need(act, q_stacked, a.block(16 * len(Q_PARTS), 0))
                nc.scalar.copy(qp[:, 0, half, :], ps[0:HC, bank_of("q", a, 0), :]).then_inc(q_h, 1)

            def qm(a, _):
                act.wait_ge(q_r, a.n(1, 1))
                nc.scalar.copy(qp[:, 1, a.base % 2, :], qr[:, :]).then_inc(q_m, 1)

            def kh(a, _):
                act.wait_ge(k_mask, a.block(1, 1))
                need(act, k_stacked, a.block(16 * len(K_PARTS), 0))
                nc.scalar.copy(kp[:, 0, :, :, :].rearrange("p a b c -> p (a b c)"), kmk[:, :, :, :].rearrange("p a b c -> p (a b c)")).then_inc(k_h, 1)

            def km(a, _):
                act.wait_ge(k_r, a.block(1, 1))
                nc.scalar.copy(kp[:, 1, :, :, :].rearrange("p a b c -> p (a b c)"), krem[:, :, :, :].rearrange("p a b c -> p (a b c)")).then_inc(k_m, 1)

            def exp(a, c):
                m = M2[a.layer]
                act.wait_ge(st_ps, a.n(5, c + 1))
                if c == 0:
                    need(act, core_done, a.n(1, -1))
                nc.scalar.activation(pt[0:m, a.base % 2, 2 * c:2 * c + 2, :].rearrange("p a b -> p (a b)"),
                                     ps[0:m, 2 + (a.base + c) % 2, :], ACT.Exp, scale=SCALE).then_inc(exp_done, 1)

            def rsq(a, _):
                act.wait_ge(ip_q2, a.n(1, 1))
                nc.scalar.activation(e40[:, 2, :], e40[:, 1, :], ACT.Ln).then_inc(act_chain, 1)
                act.wait_ge(act_chain, a.n(1, 2))
                nc.scalar.activation(e40[:, 3, :], e40[:, 2, :], ACT.Exp, scale=-0.5).then_inc(ip_rsq, 1)

            def ipe(a, _):
                act.wait_ge(ip_less, a.n(1, 1))
                nc.scalar.activation(e160[:, 2, :, :], e160[:, 1, :, :], ACT.Exp).then_inc(ip_exp, 1)

            def mtev(a, _):
                act.wait_ge(mt_ps, a.n(1, 1))
                need(act, m_stacked[a.base % 2], a.block(16, 0))
                nc.scalar.copy(mt[:, a.base % 2, :], ps[0:4 * PAIRS, bank_of("mt", a, 0), 0:S]).then_inc(mt_sb, 1)

            def ztev(a, _):
                act.wait_ge(zt_ps, a.n(1, 1))
                need(act, y_ps, a.n(1, 0))
                bank = bank_of("zt", a, 0)
                if a.layer == 0:
                    nc.scalar.copy(zt[:, 0, :], ps[:, bank, 0:S])
                    nc.scalar.copy(zt[0:Z1, 1, :], ps[0:Z1, bank, S:2 * S]).then_inc(zt_sb, 1)
                else:
                    nc.scalar.copy(zt[0:HC, :, :], ps[0:HC, bank, :].rearrange("p (a b) -> p a b", a=2)).then_inc(zt_sb, 1)

            run(ACT_STEP, {"otev": otev, "qh": qh, "qm": qm, "kh": kh, "km": km, "exp": exp, "rsq": rsq, "ipe": ipe,
                           "mtev": mtev, "ztev": ztev, "setup": setup, "iplen": iplen, "keys1": keys1})(act)

        @block.vector
        def _(dve):
            nc.vector.memset(wt[:, 0, 0:2, :], 0.0).then_inc(wt_zeroed, 1)
            for n in range(2):
                nc.vector.memset(vb[n][:, :, :, :], 0.0).then_inc(zeroed, 1)
            nc.vector.memset(vpb[:, :, :, 0:IP_ROW], 0.0).then_inc(zeroed, 1)
            dve.wait_ge(c_in[0], 32)
            dve.wait_ge(c_in[1], 16)
            ipc = ca[:, :, :].rearrange("p k (b t) -> p k b t", t=T)[:, :, :, T - N_IP:]
            for e in range(KE):
                last = nc.vector.tensor_tensor(ipsq[:, e, :].rearrange("p (b t) -> p b t", t=N_IP), ipc[:, e], ipc[:, e], ALU.mult)
            last.then_inc(sq_made, 1)
            dve.wait_ge(w_in, 32)
            dve.wait_ge(zeroed, 3)
            for n, col in ((0, C_MHH0), (1, C_MHH1)):
                for ring in range(2):
                    nc.vector.tensor_copy(vb[n][:, ring, :, SUM0:SUM0 + 2],
                                          cst[0:M2[n], col:col + 2].unsqueeze(1).broadcast_to([M2[n], PAIRS, 2])).then_inc(vsum, 1)

            def qr_(a, _):
                half = a.base % 2
                dve.wait_ge(q_h, a.n(1, 1))
                need(dve, q_l, a.n(1, 0))
                nc.vector.tensor_tensor(qr[:, :], ps[0:HC, bank_of("q", a, 0), :], qp[:, 0, half, :],
                                        ALU.subtract).then_inc(q_r, 1)

            def w(a, c):
                dve.wait_ge(u_ps, a.n(5, c + 1))
                if c == 0:
                    need(dve, core_done, a.n(1, -1))
                r = a.base % 2
                nc.vector.tensor_tensor(wt[:, r, 2 * c:2 * c + 2, :].rearrange("p a b -> p (a b)"),
                                        ps[0:M2[0], 4 + (a.base + c) % 2, :],
                                        pt[0:M2[0], r, 2 * c:2 * c + 2, :].rearrange("p a b -> p (a b)"),
                                        ALU.mult).then_inc(w_done, 1)

            def on(a, tile):
                dve.wait_ge(ot_ps, a.n(2, tile + 1))
                o12 = ps[:, bank_of("ot", a, tile), 0:(PAIRS + 2) * VW_COLS].rearrange("p (a c) -> p a c", c=VW_COLS)
                o = o12[:, 0:PAIRS, :]
                if tile == 0:
                    need(dve, z_made, a.n(2, 0))
                nc.vector.reciprocal(rs[:, tile, :, :], o[:, :, SUM0:SUM0 + 2]).then_inc(r_made, 1)
                if a.layer == 0:
                    need(dve, ip_fused, a.n(1, 0))
                    nc.vector.tensor_copy(stat[:, tile, :, 0:10], o[:, :, NUM0:NUM0 + 10])
                    own = PAIRS - 2
                    nc.vector.tensor_copy(stat[:, tile, 0:own, 10:12], o[:, 0:own, QUAD0:QUAD0 + 2])
                    nc.vector.tensor_copy(stat[:, tile, own:, 10:12], o12[:, PAIRS:, QUAD0:QUAD0 + 2]).then_inc(stat_made, 1)
                need(dve, zt_ps, a.n(1, -1))
                dve.wait_ge(r_made, a.n(2, tile + 1))
                nc.vector.tensor_tensor(z[:, a.base % 2, tile, 0:C].rearrange("p (a b c) -> p a b c", b=2, c=D),
                                        o[:, :, 0:R].rearrange("p a (b c) -> p a b c", c=D),
                                        rs[:, tile, :, :].unsqueeze(3).broadcast_to([128, PAIRS, 2, D]),
                                        ALU.mult).then_inc(z_made, 1)

            def red(a, f):
                nt = NT[a.layer]
                dve.wait_ge(sc_ps, a.n(5, f + 1))
                if f == 0:
                    need(dve, m_lo, a.n(1, 0))
                parts = [(f // 2, 4 * (f % 2), 4, 0)] if f < 4 else [(0, 8, 2, 0), (1, 8, 2, 256)]
                for tile, p0, np_, c0 in parts:
                    o = ps[:, bank_of("sc", a, f), c0:c0 + np_ * 128].rearrange("p (a c) -> p a c", c=128)
                    if a.layer == 0:
                        nc.vector.tensor_copy(ipraw[:, a.base % 4, tile, p0:p0 + np_, :], o[:, :, M2[0]:128])
                    nc.vector.tensor_reduce(mx[:, tile, p0:p0 + np_, :],
                                            o[:, :, 0:2 * nt].rearrange("p a (h t) -> p a h t", t=nt),
                                            AX_X, ALU.max).then_inc(red_done, 1)

            def neg(a, _):
                dve.wait_ge(red_done, a.n(6, 6))
                need(dve, mt_ps, a.n(1, 0))
                src = mx[:, :, :, :].rearrange("p t a h -> p t h a")
                nc.vector.tensor_scalar(mc[:, :, 0, :, :], src, -1.0, None, ALU.mult).then_inc(m_hi, 1)
                dve.wait_ge(m_hi, a.n(1, 1))
                for tile in range(2):
                    last = nc.vector.scalar_tensor_tensor(mc[:, tile, 1, :, :], src[:, tile], -1.0, mc[:, tile, 0, :, :],
                                                          ALU.mult, ALU.subtract)
                last.then_inc(m_lo, 1)

            def ipa(a, _):
                dve.wait_ge(stat_made, a.n(2, 2))
                need(dve, ip_fused, a.n(1, 0))
                nc.vector.scalar_tensor_tensor(by_head(e40[:, 0, :]), stats(8, 10), EPS2, stats(8, 10),
                                               ALU.mult, ALU.mult).then_inc(ip_least, 1)
                dve.wait_ge(ip_least, a.n(1, 1))
                nc.vector.tensor_tensor(by_head(e40[:, 1, :]), by_head(e40[:, 0, :]), stats(10, 12),
                                        ALU.max).then_inc(ip_q2, 1)
                dve.wait_ge(ip_q2, a.n(1, 1))
                nc.vector.tensor_scalar(e40[:, 0, :], e40[:, 1, :], -0.5, None, ALU.mult).then_inc(ip_half, 1)

            def ipm(a, _):
                dve.wait_ge(ip_fused, a.n(1, 1))
                nc.vector.tensor_reduce(e40[:, 7, :], e160[:, 0, :, :], AX_X, ALU.max).then_inc(ip_max, 1)

            def ipr(a, _):
                dve.wait_ge(ip_exp, a.n(1, 1))
                nc.vector.tensor_reduce(e40[:, 5, :], e160[:, 2, :, :], AX_X, ALU.add).then_inc(ip_sum, 1)
                dve.wait_ge(ip_sum, a.n(1, 1))
                nc.vector.reciprocal(e40[:, 6, :], e40[:, 5, :]).then_inc(ip_rec, 1)

            def vprep(a, _):
                m, r, lay = M2[a.layer], a.base % 2, a.layer
                dve.wait_ge(vk_ps, a.n(1, 1))
                need(dve, core_done, a.n(1, -1))
                o = ps[0:m, bank_of("vk", a, 0), SMALL0:]
                mv, v0 = (C_MV1, 0) if lay else (C_MV0, T)
                nc.vector.tensor_tensor(vb[lay][:, r, :, 0:R], o[:, v0:v0 + C].rearrange("p (a c) -> p a c", c=R),
                                        cst[0:m, mv:mv + R].unsqueeze(1).broadcast_to([m, PAIRS, R]),
                                        ALU.mult).then_inc(v_made, 1)
                if lay:
                    return
                if a.base == 0:
                    dve.wait_ge(simw_made, 1)
                need(dve, simv_made, a.n(1, 0))
                nc.vector.tensor_tensor(sim8[:, :, :], o[:, NT[0]:T].unsqueeze(1).broadcast_to([m, 2, N_IP]),
                                        simw[:, bass.ds(a.n(), 1), :, :].rearrange("p o h n -> p (o h) n"),
                                        ALU.mult).then_inc(sim_made, 1)
                nc.vector.tensor_tensor(gram[:, r, :].rearrange("p (h t) -> p h t", h=2),
                                        o[:, 0:NT[0]].unsqueeze(1).broadcast_to([m, 2, NT[0]]),
                                        cst[0:m, C_MHH0:C_MHH0 + 2].unsqueeze(2).broadcast_to([m, 2, NT[0]]),
                                        ALU.mult).then_inc(gram_made, 1)
                dve.wait_ge(sim_made, a.n(1, 1))
                nc.vector.tensor_copy(vb[0][:, r, :, NUM0:NUM0 + 8],
                                      sim8[:, :, :].rearrange("p a b -> p (a b)").unsqueeze(1).broadcast_to([m, PAIRS, 8])
                                      ).then_inc(simv_made, 1)

            def wz_(a, _):
                dve.wait_ge(vw_ps, a.n(1, 1))
                need(dve, y_ps, a.n(1, -1))
                nc.vector.tensor_tensor(wz[:, a.base % 2, :], ps[0:Z1, bank_of("vw", a, 0), SMALL0:SMALL0 + C], wrem[:, :],
                                        ALU.add).then_inc(wz_made, 1)

            def ysb(a, _):
                dve.wait_ge(y_ps, a.n(1, 1))
                bank = bank_of("y", a, 0)
                rows = bass.ds(a.n(S, -a.layer * ROWS), S)
                for mh in range(2):
                    last = nc.vector.scalar_tensor_tensor(x[:, mh, rows], ps[0:HC, bank, mh * S:(mh + 1) * S],
                                                          bo[:, a.layer, mh:mh + 1], x[:, mh, rows], ALU.add, ALU.add)
                last.then_inc(y_sb, 1)

            run(DVE_STEP, {**splits(dve, nc.vector.tensor_tensor), "qr": qr_, "w": w, "on": on, "red": red, "neg": neg, "ipa": ipa, "ipm": ipm, "ipr": ipr, "vprep": vprep,
                           "wz": wz_, "ysb": ysb})(dve)

        @block.gpsimd
        def _(pool):
            tt = nc.gpsimd.tensor_tensor
            def iplen(a, _):
                pool.wait_ge(setup_sb, 8)
                nc.gpsimd.tensor_scalar(inv[:, 0, :], inv[:, 0, :], EPS2, None, ALU.max).then_inc(inv_step, 1)
                pool.wait_ge(inv_step, 2)
                tt(inv[:, 2, :], inv[:, 1, :], inv[:, 1, :], ALU.mult).then_inc(inv_step, 1)
                pool.wait_ge(inv_step, 3)
                tt(inv[:, 2, :], inv[:, 2, :], inv[:, 0, :], ALU.mult).then_inc(inv_step, 1)
                pool.wait_ge(inv_step, 4)
                nc.gpsimd.tensor_scalar(inv[:, 2, :], inv[:, 2, :], -0.5 * SEM_SCALE, 1.5 * SEM_SCALE,
                                        ALU.mult, ALU.add).then_inc(inv_step, 1)
                pool.wait_ge(inv_step, 5)
                tt(inv[:, 3, :], inv[:, 2, :], inv[:, 1, :], ALU.mult).then_inc(inv_step, 1)
                pool.wait_ge(inv_step, 6)
                pool.wait_ge(w_in, 32)
                for hh in range(2):
                    last = nc.gpsimd.tensor_scalar(simw[:, :, hh, :], inv[0:M2[0], 3, :].rearrange("p (b n) -> p b n", n=N_IP),
                                                   cst[0:M2[0], C_MHH0 + hh:C_MHH0 + hh + 1], None, ALU.mult)
                last.then_inc(simw_made, 1)

            def linked(a, per, k, ins):
                ins.then_inc(pool_chain, 1)
                pool.wait_ge(pool_chain, a.n(per, k))

            IPC = 7

            def ipb(a, _):
                pool.wait_ge(ip_half, a.n(1, 1))
                pool.wait_ge(ip_rsq, a.n(1, 1))
                r, r2, r15 = e40[:, 3, :], e40[:, 4, :], e40[:, 2, :]
                raw = ipraw[:, a.base % 4, :, :, :].rearrange("p t a (h n) -> p (t a h) n", n=N_IP)
                ins = tt(r2, r, r, ALU.mult)
                nc.gpsimd.tensor_scalar(r15, r, 1.5, None, ALU.mult)
                nc.gpsimd.tensor_scalar(e160[:, 1, :, :], raw, SCALE, None, ALU.mult)
                linked(a, IPC, 1, ins)
                linked(a, IPC, 2, tt(r2, r2, e40[:, 0, :], ALU.mult))
                linked(a, IPC, 3, tt(r2, r2, r, ALU.mult))
                linked(a, IPC, 4, tt(r2, r2, r15, ALU.add))
                linked(a, IPC, 5, tt(e160[:, 0, :, :].rearrange("p (a h) n -> p a h n", h=2),
                                     stats(0, 8).rearrange("p a (h n) -> p a h n", h=2),
                                     by_head(r2).unsqueeze(3).broadcast_to([128, 2 * PAIRS, 2, N_IP]), ALU.mult))
                tt(e160[:, 0, :, :], e160[:, 0, :, :], e160[:, 1, :, :], ALU.add).then_inc(ip_fused, 1)

            def ipd(a, _):
                pool.wait_ge(ip_max, a.n(1, 1))
                tt(e160[:, 1, :, :], e160[:, 0, :, :], e40[:, 7, :].unsqueeze(2).broadcast_to([128, 2 * H, N_IP]),
                   ALU.subtract).then_inc(ip_less, 1)

            def ipz(a, _):
                pool.wait_ge(ip_rec, a.n(1, 1))
                if a.base == 0:
                    pool.wait_ge(rest_in, 16 * 12)
                share = e40[:, 6, :].rearrange("p (t h) -> p t h", t=2)
                linked(a, IPC, 6, tt(share, share, fside[:, :].unsqueeze(2).broadcast_to([128, 2, H]), ALU.mult))
                need(pool, zt_ps, a.n(1, -1))
                for tile in range(2):
                    ins = tt(z[:, a.base % 2, tile, C:].rearrange("p (a n) -> p a n", n=N_IP), e160[:, 2, tile * H:(tile + 1) * H, :],
                             e40[:, 6, tile * H:(tile + 1) * H].unsqueeze(2).broadcast_to([128, H, N_IP]), ALU.mult)
                    if tile:
                        ins.then_inc(ip_z, 1)
                    else:
                        linked(a, IPC, 7, ins)

            def vpb_(a, _):
                if a.base == 0:
                    pool.wait_ge(zeroed, 3)
                need(pool, vw_ps, a.n(1, -1))
                for half in range(2):
                    last = tt(vpb[:, a.base % 2, half, IP_ROW:].rearrange("p (h n) -> p h n", n=N_IP),
                              vipt[:, half, bass.ds(a.n(), 1), :].broadcast_to([HC, H, N_IP]),
                              cst[0:HC, C_MVH + half * H:C_MVH + (half + 1) * H].unsqueeze(2).broadcast_to([HC, H, N_IP]),
                              ALU.mult)
                last.then_inc(vpb_made, 1)

            run(POOL_STEP, {**splits(pool, tt), "ipb": ipb, "ipd": ipd,
                            "ipz": ipz, "vpb": vpb_, "iplen": iplen})(pool)


def kernel(x, ctx_2048, fside_S_0, L0_xattn_W_q, L0_xattn_W_k, L0_xattn_W_v, L0_xattn_W_k_ip, L0_xattn_W_v_ip,
           L0_xattn_W_out, L0_xattn_b_out, L1_xattn_Wq, L1_xattn_Wk, L1_xattn_Wv, L1_xattn_Wk_ip, L1_xattn_Wv_ip,
           L1_xattn_Wo, L1_xattn_bo):
    import concourse.bacc as bacc
    from concourse.bass_utils import run_bass_kernel_spmd

    def tiles(w, p):
        w = np.asarray(w)
        return w.reshape(-1, p, w.shape[1]).transpose(1, 0, 2)

    perm = np.arange(C).reshape(HP, 2, R).transpose(1, 2, 0).ravel()
    wq0, wq1 = np.asarray(L0_xattn_W_q)[:, perm], np.asarray(L1_xattn_Wq).T[:, perm]
    wk0, wk1 = np.asarray(L0_xattn_W_k)[:, perm], np.asarray(L1_xattn_Wk).T[:, perm]
    ctx = np.asarray(ctx_2048).transpose(0, 2, 1).reshape(B, KE, 128, T).transpose(0, 2, 1, 3)
    text = ctx[..., :NT[0]]
    wo = np.asarray(L0_xattn_W_out)
    wrem = np.zeros((Z1, C), np.float32)
    wrem[:C - 128] = wo[128:]
    consts, ones_rows, ident16 = constants()
    data = {
        "xT": np.asarray(x).reshape(ROWS, 2, HC).transpose(2, 1, 0),
        "ctxT": ctx.transpose(1, 2, 0, 3).reshape(128, KE, B * T),
        "ctx0": np.concatenate([text, text, ctx], axis=3),
        "ctx1": np.concatenate([ctx, ctx], axis=3),
        "side": np.asarray(fside_S_0).reshape(2, 128).T,
        "WQ": np.stack([tiles(wq0, HC), tiles(wq1, HC)]),
        "WK": np.stack([tiles(wk0, 128), tiles(wk1, 128)]),
        "WKIP": tiles(np.asarray(L0_xattn_W_k_ip)[:, perm], 128),
        "WV": np.stack([tiles(L0_xattn_W_v, 128), tiles(np.asarray(L1_xattn_Wv).T, 128)]),
        "WVIP": tiles(L0_xattn_W_v_ip, 128),
        "WO0": wo[:128],
        "WREM": wrem,
        "WOP": tiles(wo, HC),
        "WO1": tiles(np.asarray(L1_xattn_Wo).T, HC),
        "BO": np.stack([np.asarray(L0_xattn_b_out).reshape(2, HC).T, np.asarray(L1_xattn_bo).reshape(2, HC).T], axis=1),
        "consts": consts,
        "ones_rows": ones_rows,
        "ident16": ident16,
    }
    nc = bacc.Bacc("TRN2", target_bir_lowering=False, num_devices=1)
    arrays, args = {}, {}
    for name, a in data.items():
        a = np.ascontiguousarray(a)
        arrays["in_" + name] = a
        args[name] = nc.dram_tensor("in_" + name, a.shape, mybir.dt.from_np(a.dtype), kind="ExternalInput").ap()
    args["outT"] = nc.dram_tensor("out_T", (HC, 2, ROWS), F32, kind="ExternalOutput").ap()
    xattn_kernel(nc, **args)
    result = run_bass_kernel_spmd(nc, [arrays], core_ids=[0]).results[0]["out_T"]
    return result.transpose(2, 1, 0).reshape(B, S, C)
```
